# Optimizing a Trainium2 kernel written in Bass

```python
import numpy as np
import jax
import jax.numpy as jnp

def _softmax(x, axis=-1):
    return jax.nn.softmax(x, axis=axis)

def _gelu(x):
    return jax.nn.gelu(x, approximate=True)

def _silu(x):
    return jax.nn.silu(x)

def _sigmoid(x):
    return jax.nn.sigmoid(x)

def _layernorm(x, axis=-1, eps=1e-05):
    m = jnp.mean(x, axis=axis, keepdims=True)
    v = jnp.var(x, axis=axis, keepdims=True)
    return (x - m) / jnp.sqrt(v + eps)

def _scatter_add(tgt, idx, src, axis=0):
    return tgt.at[idx].add(src)

def _segment_sum(src, seg, n):
    return jax.ops.segment_sum(src, seg, n)
kernel_name = 'mk_gnn_preln_d1_gnn_r32_8821ce'

def setup_inputs(seed: int=0):
    np.random.seed(seed)
    _w = jnp.asarray

    def _rec_inputs():
        import jax
        import jax.numpy as jnp
        _gk = jax.random.key(seed)
        x = -0.000202 + 1 * jax.random.normal(jax.random.fold_in(_gk, 1), (50000, 128), jnp.float32)
        src = jax.random.randint(jax.random.fold_in(_gk, 2), (25000,), 0, 50000, jnp.int32)
        dst = jnp.minimum((50000 * jax.random.uniform(jax.random.fold_in(_gk, 3), (25000,)) ** 2.0).astype(jnp.int32), 49999)
        _o = jnp.argsort(dst, stable=True)
        src = src[_o]
        dst = dst[_o]
        edge_attr_32 = 0.000196303 + 1.00016 * jax.random.normal(jax.random.fold_in(_gk, 11), (25000, 32), jnp.float32)
        return (x, src, dst, edge_attr_32)
    x, src, dst, edge_attr_32 = _rec_inputs()

    def _L0_gnn_setup():
        import jax, jax.numpy as jnp
        import numpy as np
        N = 50000
        E = 25000
        NODE_DIM = 128
        EDGE_DIM = 32
        HIDDEN = 128

        def _linear_params(key, fan_in, fan_out):
            kw, kb = jax.random.split(key)
            bound = 1.0 / np.sqrt(fan_in)
            W = jax.random.uniform(kw, (fan_in, fan_out), minval=-bound, maxval=bound, dtype=jnp.float32)
            b = jax.random.uniform(kb, (fan_out,), minval=-bound, maxval=bound, dtype=jnp.float32)
            return (W, b)
        key = jax.random.key(seed)
        ks = jax.random.split(key, 7)
        h = jax.random.normal(ks[0], (N, NODE_DIM), dtype=jnp.float32)
        edge_index = jax.random.randint(ks[1], (2, E), 0, N, dtype=jnp.int64)
        edge_attr = jax.random.normal(ks[2], (E, EDGE_DIM), dtype=jnp.float32)
        Wm1, bm1 = _linear_params(ks[3], 2 * NODE_DIM + EDGE_DIM, HIDDEN)
        Wm2, bm2 = _linear_params(ks[4], HIDDEN, HIDDEN)
        Wu1, bu1 = _linear_params(ks[5], NODE_DIM + HIDDEN, HIDDEN)
        Wu2, bu2 = _linear_params(ks[6], HIDDEN, NODE_DIM)
        return {'h': h, 'edge_attr': edge_attr, 'Wm1': Wm1, 'bm1': bm1, 'Wm2': Wm2, 'bm2': bm2, 'Wu1': Wu1, 'bu1': bu1, 'Wu2': Wu2, 'bu2': bu2, 'edge_index': edge_index}
    _L0_gnn_all = _L0_gnn_setup()
    _L0_gnn_in = {k: v for k, v in _L0_gnn_all.items() if k in ('Wm1', 'bm1', 'Wm2', 'bm2', 'Wu1', 'bu1', 'Wu2', 'bu2')}
    del _L0_gnn_all
    return {'x': x, 'src': src, 'dst': dst, 'edge_attr_32': edge_attr_32, 'L0_gnn_Wm1': _L0_gnn_in['Wm1'], 'L0_gnn_bm1': _L0_gnn_in['bm1'], 'L0_gnn_Wm2': _L0_gnn_in['Wm2'], 'L0_gnn_bm2': _L0_gnn_in['bm2'], 'L0_gnn_Wu1': _L0_gnn_in['Wu1'], 'L0_gnn_bu1': _L0_gnn_in['bu1'], 'L0_gnn_Wu2': _L0_gnn_in['Wu2'], 'L0_gnn_bu2': _L0_gnn_in['bu2']}

def reference(x, src, dst, edge_attr_32, L0_gnn_Wm1, L0_gnn_bm1, L0_gnn_Wm2, L0_gnn_bm2, L0_gnn_Wu1, L0_gnn_bu1, L0_gnn_Wu2, L0_gnn_bu2):
    import jax
    import jax.numpy as jnp

    def _L0_gnn_ref(h, edge_attr, Wm1, bm1, Wm2, bm2, Wu1, bu1, Wu2, bu2, edge_index):
        import jax, jax.numpy as jnp
        import numpy as np
        N = 50000
        E = 25000
        NODE_DIM = 128
        EDGE_DIM = 32
        HIDDEN = 128

        def _linear_params(key, fan_in, fan_out):
            kw, kb = jax.random.split(key)
            bound = 1.0 / np.sqrt(fan_in)
            W = jax.random.uniform(kw, (fan_in, fan_out), minval=-bound, maxval=bound, dtype=jnp.float32)
            b = jax.random.uniform(kb, (fan_out,), minval=-bound, maxval=bound, dtype=jnp.float32)
            return (W, b)
        src = edge_index[0]
        dst = edge_index[1]
        msg_input = jnp.concatenate([h[src], h[dst], edge_attr], axis=-1)
        x = jax.nn.relu(msg_input @ Wm1 + bm1)
        messages = jax.nn.relu(x @ Wm2 + bm2)
        agg = jax.ops.segment_sum(messages, dst, num_segments=N)
        update_input = jnp.concatenate([h, agg], axis=-1)
        u = jax.nn.relu(update_input @ Wu1 + bu1)
        h_new = h + (u @ Wu2 + bu2)
        return h_new
    edge_index = jnp.stack([src, dst])
    h = jnp.maximum(_layernorm(x, axis=-1), 0.0)
    x = x + _L0_gnn_ref(h, edge_attr_32, L0_gnn_Wm1, L0_gnn_bm1, L0_gnn_Wm2, L0_gnn_bm2, L0_gnn_Wu1, L0_gnn_bu1, L0_gnn_Wu2, L0_gnn_bu2, edge_index)
    return x

_drawn_inputs = setup_inputs


def setup_inputs(seed=0):
    import zlib

    import numpy as np

    out = dict(_drawn_inputs(seed))
    spreads = {}
    factors = {'edge_attr_32': 8.0,
     'L0_gnn_Wm1': 6.792,
     'L0_gnn_bm1': 25.389,
     'L0_gnn_Wm2': 4.96,
     'L0_gnn_bm2': 33.164,
     'L0_gnn_bu1': 6.228,
     'L0_gnn_bu2': 4.107}
    for name, (base, spread) in spreads.items():
        noise = np.random.default_rng([zlib.crc32(name.encode()), seed]).standard_normal(out[name].shape)
        drawn = base * np.exp(spread * noise) if base else spread * noise
        out[name] = jnp.asarray(drawn.astype(out[name].dtype))
    for name, factor in factors.items():
        out[name] = (out[name] * factor).astype(out[name].dtype)
    return out
```

```python
from contextlib import ExitStack

import numpy as np

import concourse.bass as bass
from concourse import mybir

F32 = mybir.dt.float32
I32 = mybir.dt.int32
ALU = mybir.AluOpType
ACT = mybir.ActivationFunctionType
AX_X = mybir.AxisListType.X

P = 128
N, E, D, DE = 50000, 25000, 128, 32
W = 4 * P
STEPS = -(-E // W)
ET = 4 * STEPS
GROUPS = -(-N // W)
LAST = N - W
NEW = (GROUPS - 1) * W
EPS = 1e-5
STAT = 12
TABLE = 23
assert GROUPS == 2 * STEPS


def run_steps(eng, total, first, last, unroll, body):
    first, last = -(-first // unroll) * unroll, last // unroll * unroll
    for s in range(first):
        body(s, s % unroll, s // unroll)
    with eng.Fori(first // unroll, last // unroll) as use:
        for slot in range(unroll):
            body(use * unroll + slot, slot, use)
    for s in range(last, total):
        body(s, s % unroll, s // unroll)


def at_least(s, k):
    return not isinstance(s, int) or s >= k


def below(s, k):
    return not isinstance(s, int) or s < k


def build(nc, x, ends, dst_rows, dst_cols, edge_t, wm1, bm1, wm2, bm2, wu1, bu1, wu2, bu2, out):
    with ExitStack() as ctx:
        def sb(name, shape, dt=F32):
            return ctx.enter_context(nc.sbuf_tensor(name, shape, dt))

        def ps(name, shape, dt=F32):
            return ctx.enter_context(nc.psum_tensor(name, shape, dt))

        def sem(name):
            return ctx.enter_context(nc.semaphore(name))

        hu_d = nc.dram_tensor("hu_scratch", (GROUPS, P, W), F32).ap()
        xh_d = nc.dram_tensor("xh_scratch", (GROUPS, P, W), F32).ap()
        ext_d = nc.dram_tensor("extremes_scratch", (2, ET), F32).ap()
        rng_d = nc.dram_tensor("ranges_scratch", (GROUPS, 8), I32).ap()

        w_src, w_dst, w_msg = sb("w_src", [P, D]), sb("w_dst", [P, D]), sb("w_msg", [P, D])
        w_edge = sb("w_edge", [DE, D])
        w_uh, w_ua, w_out = sb("w_uh", [P, D]), sb("w_ua", [P, D]), sb("w_out", [P, D])
        b_m1, b_m2, b_u1 = sb("b_m1", [P, 1]), sb("b_m2", [P, 1]), sb("b_u1", [P, 1])
        b_out = sb("b_out", [P, W])
        ident = sb("ident", [P, P])
        ends_all = sb("ends_all", [P, STEPS, 8], I32)
        ends_now = sb("ends_now", [P, 4, 8], I32)
        dst_i = sb("dst_i", [P, ET + 1], I32)
        dst_f = sb("dst_f", [P, ET + 1])

        rows_i = sb("rows_i", [ET // 2, 2, P], I32)
        rows_f = sb("rows_f", [ET // 2, 2, P])
        ext = sb("ext", [ET // 2, 2, 2])
        ranges = sb("ranges", [1, GROUPS * 8], I32)
        base_i, cap_i = sb("base_i", [GROUPS, 4], I32), sb("cap_i", [GROUPS, 4], I32)
        base_f, cap_f, top_f = sb("base_f", [GROUPS, 4]), sb("cap_f", [GROUPS, 4]), sb("top_f", [GROUPS, 4])
        up_i, down_i = sb("up_i", [P, ET], I32), sb("down_i", [P, ET], I32)
        lo_f, hi_f = sb("lo_f", [GROUPS, 4]), sb("hi_f", [GROUPS, 4])
        rng_i = sb("rng_i", [GROUPS, 4, 2], I32)

        msgs = sb("msgs", [P, ET + 1, D])
        xg = sb("xg", [P, 2, 8, D])
        xn = sb("xn", [P, 2, 8, D])
        edge = sb("edge", [DE, 2, W])
        bn = sb("bn", [P, 16, 6])
        pair, diff = sb("pair", [P, 16, 2]), sb("diff", [P, 16])
        sq, mean, var, sd = sb("sq", [P, 16]), sb("mean", [P, 16]), sb("var", [P, 16]), sb("sd", [P, 16])
        veps, r0, r1, r2 = sb("veps", [P, 16]), sb("r0", [P, 16]), sb("r1", [P, 16]), sb("r2", [P, 16])
        rstd, shift = sb("rstd", [P, 16]), sb("shift", [P, 16])
        z = sb("z", [P, 2, 16, D])
        ht = sb("ht", [P, 2, 4, W])
        m1t, m2t = sb("m1t", [P, W]), sb("m2t", [P, W])
        hu_o = sb("hu_o", [P, 2, 2, W])
        xh_o = sb("xh_o", [P, 2, 2, W])

        ext_all = z[:, 0, :, :].rearrange("p t d -> p (t d)")[:, 0:2 * ET].rearrange("p (a k) -> p a k", a=2)
        up_f = z[:, 0, :, :].rearrange("p t d -> p (t d)")[:, 512:512 + ET]
        down_f = z[:, 0, :, :].rearrange("p t d -> p (t d)")[:, 768:768 + ET]
        below_mx = z[0:GROUPS, 1, 0:8, :].rearrange("p t d -> p (t d)")[:, 0:4 * ET].rearrange("p (c k) -> p c k", c=4)
        hit = z[0:GROUPS, 1, 8:16, :].rearrange("p t d -> p (t d)")[:, 0:4 * ET].rearrange("p (c k) -> p c k", c=4)
        score = ht[0:GROUPS, 0, 0:2, :].rearrange("p t d -> p (t d)")[:, 0:4 * ET].rearrange("p (c k) -> p c k", c=4)
        score2 = ht[0:GROUPS, 1, 0:2, :].rearrange("p t d -> p (t d)")[:, 0:4 * ET].rearrange("p (c k) -> p c k", c=4)

        hot_a = z[:, 0, :, :].rearrange("p (u j) d -> p u j d", u=4)[:, 0:2]
        hot_b = z[:, 0, :, :].rearrange("p (u j) d -> p u j d", u=4)[:, 2:4]
        ids = z[:, 1, :, :].rearrange("p (u j) d -> p u (j d)", u=4)[:, 0:2]
        hop = m1t[:]
        hu_i = ht[:, 0, :, :]
        xh_i = ht[:, 1, :, :]
        u_n = xg[:, 0, :, :].rearrange("p (u j) d -> p u (j d)", u=2)
        u_t = xg[:, 1, :, :].rearrange("p (u j) d -> p u (j d)", u=2)
        out_o = xn[:, :, :, :].rearrange("p a (u j) d -> p (a u) (j d)", u=2)

        banks = [ps(f"bank{i}", [P, W]) for i in range(8)]
        p_tr, (p_m1, p_m2, p_msg, p_hu) = banks[0:4], banks[4:8]
        p_agg, p_ut, p_out = banks[0:2], banks[2:4], banks[4:6]

        s_w = sem("weights_loaded")
        s_idx = sem("indices_loaded")
        s_cst = sem("constants_made")
        s_pre = sem("table_steps")
        s_ext = sem("extremes_moved")
        s_rng = sem("ranges_moved")
        s_xn = [sem(f"nodes_loaded{i}") for i in range(2)]
        s_xg = [sem(f"ends_gathered{i}") for i in range(2)]
        s_cp = sem("ends_copied")
        s_stat = sem("stat")
        s_sd = sem("sd_ready")
        s_zv = sem("z_by_vector")
        s_za = sem("z_by_scalar")
        s_xh = sem("xh_ready")
        s_tr = sem("transposed")
        s_ht = sem("ht_ready")
        s_m1, s_m2, s_msg, s_hu = sem("m1_summed"), sem("m2_summed"), sem("msg_summed"), sem("hu_summed")
        s_m1t, s_m2t, s_msgs, s_huo = sem("m1t_ready"), sem("m2t_ready"), sem("msgs_ready"), sem("hu_ready")
        s_sto = [sem(f"scratch_stored{i}") for i in range(2)]

        s_ld = [sem(f"scratch_loaded{i}") for i in range(4)]
        s_hop = sem("hop_made")
        s_ids = sem("ids_ready")
        s_a = sem("first_onehots_ready")
        s_b = [sem(f"more_onehots_ready{j}") for j in range(4)]
        s_bu = [sem(f"more_onehots_used{j}") for j in range(4)]
        s_un = sem("u_ready")
        s_t2 = sem("u_transposed")
        s_ut = sem("ut_ready")
        s_xb = sem("xh_biased")
        s_o = sem("out_summed")
        s_fin = sem("out_ready")
        s_out = [sem(f"out_stored{i}") for i in range(4)]

        def sync_1(sp):
            sp.dma_start(ends_all[:], ends).then_inc(s_idx, 16)
            sp.dma_start(rows_i[:], dst_rows).then_inc(s_ext, 16)

            def load_nodes(s, slot):
                if below(s, STEPS - 1):
                    sp.dma_start(xn[:, slot], x[bass.ds(s * 2 * W, 2 * W), :].rearrange("(j p) d -> p j d", p=P)
                                 ).then_inc(s_xn[slot], 16)
                else:
                    for h, row in enumerate((s * 2 * W, LAST)):
                        sp.dma_start(xn[:, slot, 4 * h:4 * h + 4],
                                     x[row:row + W, :].rearrange("(j p) d -> p j d", p=P)).then_inc(s_xn[slot], 16)
                sp.dma_start(edge[:, slot], edge_t[:, bass.ds(s * W, W)]).then_inc(s_xn[slot], 16)

            load_nodes(0, 0)
            sp.dma_start(dst_i[:], dst_cols).then_inc(s_ext, 16)
            for to, of in ((w_src, wm1[0:D]), (w_dst, wm1[D:2 * D]), (w_edge, wm1[2 * D:2 * D + DE]), (w_msg, wm2),
                           (w_uh, wu1[0:D]), (w_ua, wu1[D:2 * D]), (w_out, wu2),
                           (b_m1, bm1), (b_m2, bm2), (b_u1, bu1), (b_out, bu2)):
                sp.dma_start(to[:], of).then_inc(s_w, 16)
            load_nodes(1, 1)
            sp.wait_ge(s_pre, 3)
            for a in range(2):
                sp.dma_start(ext_d[a].rearrange("(q k) -> q k", k=2), ext[:, a, :]).then_inc(s_ext, 16)
            sp.wait_ge(s_ext, 64)
            for a in range(2):
                sp.dma_start(ext_all[:, a, :], ext_d[a].partition_broadcast(P)).then_inc(s_ext, 16)
            sp.wait_ge(s_pre, TABLE)
            sp.dma_start(rng_d, rng_i[:].rearrange("g c a -> g (c a)")).then_inc(s_rng, 16)
            sp.wait_ge(s_rng, 16)
            sp.dma_start(ranges[:], rng_d.rearrange("(o g) c -> o (g c)", o=1)).then_inc(s_rng, 16)

            def body(s, slot, use):
                if below(s, STEPS) and at_least(s, 2):
                    sp.wait_ge(s_xh, 2 * (s - 1))
                    sp.wait_ge(s_m1, s - 1)
                    load_nodes(s, slot)
                if at_least(s, 2):
                    to = bass.ds(2 * (s - 2), 2)
                    sp.wait_ge(s_xh, 2 * (s - 1))
                    sp.dma_start(xh_d[to].rearrange("g p f -> p g f"), xh_o[:, slot]).then_inc(s_sto[slot], 16)
                    sp.wait_ge(s_huo, 2 * (s - 1))
                    sp.dma_start(hu_d[to].rearrange("g p f -> p g f"), hu_o[:, slot]).then_inc(s_sto[slot], 16)

            run_steps(sp, STEPS + 2, 2, STEPS - 1, 2, body)
            sp.wait_ge(s_rng, 32)
            for slot in range(2):
                sp.wait_ge(s_sto[slot], 32 * ((STEPS + 1 - slot) // 2))

        def gpsimd_1(pool):
            pool.memset(ident[:], 0.0).then_inc(s_cst, 1)
            pool.wait_ge(s_cst, 1)
            pool.affine_select(out=ident[:], in_=ident[:], compare_op=ALU.not_equal, fill=1.0, base=0,
                               pattern=[[-1, P]], channel_multiplier=1).then_inc(s_cst, 1)
            pool.iota(base_i[:], [[P, 4]], base=0, channel_multiplier=W).then_inc(s_cst, 1)
            pool.iota(cap_i[:], [[P, 4]], base=LAST, channel_multiplier=0).then_inc(s_cst, 1)
            pool.iota(up_i[:], [[1, ET]], base=1, channel_multiplier=0).then_inc(s_cst, 1)
            pool.iota(down_i[:], [[-1, ET]], base=ET, channel_multiplier=0).then_inc(s_cst, 1)
            pool.memset(msgs[:, ET, :], 0.0).then_inc(s_cst, 1)
            pool.wait_ge(s_idx, 16)

            pool.tensor_copy(ends_now[:, 0], ends_all[:, 0, :]).then_inc(s_cp, 1)

            def body(s, slot, use):
                pool.wait_ge(s_cp, s + 1)
                if at_least(s, 2):
                    pool.wait_ge(s_zv, 3 * s - 4)
                if below(s, STEPS - 1):
                    pool.tensor_copy(ends_now[:, (slot + 1) % 4], ends_all[:, s + 1, :]).then_inc(s_cp, 1)
                for t in range(8):
                    pool.indirect_dma_start(
                        xg[:, slot % 2, t, :], None, x,
                        bass.IndirectOffsetOnAxis(ap=ends_now[:, slot, t:t + 1], axis=0)).then_inc(s_xg[slot % 2], 16)

            run_steps(pool, STEPS, 2, STEPS - 1, 4, body)

        def table_of_ranges(dve):
            n = [0]

            def did(ins, wait=True):
                n[0] += 1
                ins.then_inc(s_pre, 1)
                if wait:
                    dve.wait_ge(s_pre, n[0])

            dve.wait_ge(s_ext, 32)
            did(dve.tensor_copy(rows_f[:], rows_i[:]))
            did(dve.tensor_reduce(ext[:, 0, :], rows_f[:], AX_X, ALU.min), False)
            did(dve.tensor_reduce(ext[:, 1, :], rows_f[:], AX_X, ALU.max), False)
            did(dve.tensor_copy(dst_f[:], dst_i[:]), False)
            dve.wait_ge(s_cst, 7)
            did(dve.tensor_copy(base_f[:], base_i[:]), False)
            did(dve.tensor_copy(cap_f[:], cap_i[:]), False)
            did(dve.tensor_copy(up_f, up_i[:]), False)
            did(dve.tensor_copy(down_f, down_i[:]))
            did(dve.tensor_tensor(base_f[:], base_f[:], cap_f[:], ALU.min))
            did(dve.tensor_scalar(top_f[:], base_f[:], float(P - 1), None, ALU.add))
            dve.wait_ge(s_ext, 96)
            for c in range(4):
                did(dve.tensor_scalar(below_mx[:, c, :], ext_all[0:GROUPS, 1, :], base_f[:, c:c + 1], None, ALU.is_ge))
                ins = dve.scalar_tensor_tensor(out=hit[:, c, :], in0=ext_all[0:GROUPS, 0, :], scalar=top_f[:, c:c + 1],
                                               in1=below_mx[:, c, :], op0=ALU.is_le, op1=ALU.mult)
                if c == 3:
                    did(ins)
            did(dve.tensor_tensor(score[:], hit[:], up_f[0:GROUPS].unsqueeze(1).broadcast_to([GROUPS, 4, ET]),
                                  ALU.mult), False)
            did(dve.tensor_tensor(score2[:], hit[:], down_f[0:GROUPS].unsqueeze(1).broadcast_to([GROUPS, 4, ET]),
                                  ALU.mult))
            did(dve.tensor_reduce(hi_f[:], score[:], AX_X, ALU.max), False)
            did(dve.tensor_reduce(lo_f[:], score2[:], AX_X, ALU.max))
            did(dve.tensor_scalar(lo_f[:], lo_f[:], -1.0, float(ET), ALU.mult, ALU.add))
            did(dve.tensor_scalar(lo_f[:], lo_f[:], float(ET - 1), None, ALU.min))
            did(dve.scalar_tensor_tensor(out=hi_f[:], in0=lo_f[:], scalar=1.0, in1=hi_f[:], op0=ALU.add, op1=ALU.max),
                False)
            dve.tensor_copy(rng_i[:, :, 0], lo_f[:])
            dve.wait_ge(s_pre, n[0])
            did(dve.tensor_copy(rng_i[:, :, 1], hi_f[:]))
            assert n[0] == TABLE

        VECTOR_TILES = 10

        def vector_1(dve):
            table_of_ranges(dve)

            def stats(s, slot, use):
                if at_least(s, 1):
                    dve.wait_ge(s_zv, 3 * s)
                dve.wait_ge(s_xn[slot], 32 * use + 32 + (0 if below(s, STEPS - 1) else 16))
                for t in range(8):
                    dve.bn_stats(bn[:, 8 + t, :], xn[:, slot, t, :])
                dve.wait_ge(s_xg[slot], 128 * use + 128)
                for t in range(8):
                    ins = dve.bn_stats(bn[:, t, :], xg[:, slot, t, :])
                ins.then_inc(s_stat, 1)
                dve.wait_ge(s_stat, STAT * s + 1)
                dve.tensor_tensor(pair[:], bn[:, :, 1:3], bn[:, :, 4:6], ALU.add).then_inc(s_stat, 1)
                dve.tensor_tensor(diff[:], bn[:, :, 1], bn[:, :, 4], ALU.subtract).then_inc(s_stat, 1)
                dve.wait_ge(s_stat, STAT * s + 3)
                dve.scalar_tensor_tensor(out=sq[:], in0=diff[:], scalar=0.25, in1=diff[:], op0=ALU.mult,
                                         op1=ALU.mult).then_inc(s_stat, 1)
                dve.tensor_scalar(mean[:], pair[:, :, 0], 0.5, None, ALU.mult).then_inc(s_stat, 1)
                dve.wait_ge(s_stat, STAT * s + 5)
                dve.scalar_tensor_tensor(out=var[:], in0=pair[:, :, 1], scalar=1.0 / D, in1=sq[:], op0=ALU.mult,
                                         op1=ALU.add).then_inc(s_stat, 1)
                dve.wait_ge(s_stat, STAT * s + 6)
                dve.tensor_scalar(veps[:], var[:], EPS, None, ALU.add).then_inc(s_stat, 1)

            def x_plus_h(s, slot, use):
                dve.wait_ge(s_za, 2 * s + 2)
                dve.wait_ge(s_zv, 3 * s + 3)
                if at_least(s, 2):
                    dve.wait_ge(s_sto[slot], 32 * use)
                for h in range(2):
                    dve.scalar_tensor_tensor(
                        out=xh_o[:, slot, h, :].rearrange("p (j d) -> p j d", j=4), in0=z[:, slot, 8 + 4 * h:12 + 4 * h, :],
                        scalar=0.0, in1=xn[:, slot, 4 * h:4 * h + 4, :], op0=ALU.max, op1=ALU.add).then_inc(s_xh, 1)

            def normalise(s, slot, use):
                dve.wait_ge(s_sd, s + 1)
                dve.reciprocal(r0[:], sd[:]).then_inc(s_stat, 1)
                dve.wait_ge(s_stat, STAT * s + 8)
                dve.scalar_tensor_tensor(out=r1[:], in0=r0[:], scalar=-0.5, in1=r0[:], op0=ALU.mult,
                                         op1=ALU.mult).then_inc(s_stat, 1)
                dve.wait_ge(s_stat, STAT * s + 9)
                dve.tensor_tensor(r2[:], r1[:], veps[:], ALU.mult).then_inc(s_stat, 1)
                dve.wait_ge(s_stat, STAT * s + 10)
                dve.scalar_tensor_tensor(out=rstd[:], in0=r2[:], scalar=1.5, in1=r0[:], op0=ALU.add,
                                         op1=ALU.mult).then_inc(s_stat, 1)
                dve.wait_ge(s_stat, STAT * s + 11)
                dve.scalar_tensor_tensor(out=shift[:], in0=mean[:], scalar=-1.0, in1=rstd[:], op0=ALU.mult,
                                         op1=ALU.mult).then_inc(s_stat, 1)
                if at_least(s, 2):
                    dve.wait_ge(s_tr, 4 * (s - 1))
                    dve.wait_ge(s_xh, 2 * (s - 1))
                for t in range(VECTOR_TILES):
                    of = xg[:, slot, t, :] if t < 8 else xn[:, slot, t - 8, :]
                    ins = dve.tensor_scalar(z[:, slot, t, :], of, mean[:, t:t + 1], rstd[:, t:t + 1],
                                            ALU.subtract, ALU.mult)
                    if t in (3, 7, VECTOR_TILES - 1):
                        ins.then_inc(s_zv, 1)

            def body(s, slot, use):
                if below(s, STEPS):
                    stats(s, slot, use)
                if at_least(s, 1):
                    x_plus_h(s - 1, 1 - slot, use - (1 - slot))
                if below(s, STEPS):
                    normalise(s, slot, use)

            run_steps(dve, STEPS + 1, 3, STEPS - 1, 2, body)

        def scalar_1(act):
            act.wait_ge(s_w, 16 * 11)

            def body(s, slot, use):
                if below(s, STEPS):
                    act.wait_ge(s_stat, STAT * s + 7)
                    act.activation(sd[:], veps[:], ACT.Sqrt).then_inc(s_sd, 1)
                if at_least(s, 1):
                    e, eslot, euse = s - 1, 1 - slot, use - (1 - slot)
                    act.wait_ge(s_m1, e + 1)
                    act.activation(m1t[:], p_m1[:], ACT.Relu, bias=b_m1[:]).then_inc(s_m1t, 1)
                    if at_least(e, 2):
                        act.wait_ge(s_sto[eslot], 32 * euse)
                    act.wait_ge(s_hu, 2 * e + 1)
                    act.activation(hu_o[:, eslot, 0, :], p_hu[:], ACT.Copy).then_inc(s_huo, 1)
                    act.wait_ge(s_m2, e + 1)
                    act.activation(m2t[:], p_m2[:], ACT.Relu, bias=b_m2[:]).then_inc(s_m2t, 1)
                    act.wait_ge(s_hu, 2 * e + 2)
                    act.activation(hu_o[:, eslot, 1, :], p_hu[:], ACT.Copy).then_inc(s_huo, 1)
                    act.wait_ge(s_msg, e + 1)
                    act.activation(msgs[:, bass.ds(4 * e, 4), :], p_msg[:].rearrange("p (j d) -> p j d", j=4),
                                   ACT.Copy).then_inc(s_msgs, 1)
                if below(s, STEPS):
                    act.wait_ge(s_stat, STAT * s + 12)
                    for t in range(VECTOR_TILES, 16):
                        ins = act.activation(z[:, slot, t, :], xn[:, slot, t - 8, :], ACT.Identity,
                                             bias=shift[:, t:t + 1], scale=rstd[:, t:t + 1])
                        if t in (11, 15):
                            ins.then_inc(s_za, 1)
                    for q in range(4):
                        act.wait_ge(s_tr, 4 * s + q + 1)
                        act.activation(ht[:, slot, q, :], p_tr[q][:], ACT.Relu).then_inc(s_ht, 1)

            run_steps(act, STEPS + 1, 3, STEPS - 1, 2, body)

        def tensor_1(pe):
            pe.wait_ge(s_w, 16 * 11)
            pe.wait_ge(s_cst, 2)

            def edges_and_nodes(s, slot, use):
                pe.wait_ge(s_ht, 4 * s + 2)
                pe.wait_ge(s_xn[slot], 32 * use + 32 + (0 if below(s, STEPS - 1) else 16))
                if at_least(s, 1):
                    pe.wait_ge(s_m1t, s)
                pe.matmul(p_m1[:], w_src[:], ht[:, slot, 0, :], start=True, stop=False)
                pe.matmul(p_m1[:], w_dst[:], ht[:, slot, 1, :], start=False, stop=False)
                pe.matmul(p_m1[:], w_edge[:], edge[:, slot, :], start=False, stop=True).then_inc(s_m1, 1)
                for h in range(2):
                    pe.wait_ge(s_ht, 4 * s + 3 + h)
                    if h == 1 or at_least(s, 1):
                        pe.wait_ge(s_huo, 2 * s + h)
                    for j in range(4):
                        ins = pe.matmul(p_hu[:, j * D:(j + 1) * D], ht[:, slot, 2 + h, j * P:(j + 1) * P], w_uh[:],
                                        start=True, stop=True)
                    ins.then_inc(s_hu, 1)
                    if h == 0:
                        pe.wait_ge(s_m1t, s + 1)
                        pe.matmul(p_m2[:], w_msg[:], m1t[:], start=True, stop=True).then_inc(s_m2, 1)
                pe.wait_ge(s_m2t, s + 1)
                if at_least(s, 1):
                    pe.wait_ge(s_msgs, s)
                for j in range(4):
                    ins = pe.matmul(p_msg[:, j * D:(j + 1) * D], m2t[:, j * P:(j + 1) * P], w_ua[:],
                                    start=True, stop=True)
                ins.then_inc(s_msg, 1)

            def transposes(s, slot, use):
                for q in range(4):
                    pe.wait_ge(s_zv, 3 * s + min(q, 2) + 1)
                    if q >= 2:
                        pe.wait_ge(s_za, 2 * s + q - 1)
                    if at_least(s, 1):
                        pe.wait_ge(s_ht, 4 * (s - 1) + q + 1)
                    for j in range(4):
                        ins = pe.transpose(p_tr[q][:, j * P:(j + 1) * P], z[:, slot, 4 * q + j, :], ident[:])
                    ins.then_inc(s_tr, 1)

            def body(s, slot, use):
                if at_least(s, 1):
                    edges_and_nodes(s - 1, 1 - slot, use - (1 - slot))
                if below(s, STEPS):
                    transposes(s, slot, use)

            run_steps(pe, STEPS + 1, 3, STEPS - 1, 2, body)

        with nc.Block() as block:
            block.sync(sync_1)
            block.gpsimd(gpsimd_1)
            block.vector(vector_1)
            block.scalar(scalar_1)
            block.tensor(tensor_1)

        def sync_2(sp):
            def store(g, slot, use):
                sp.wait_ge(s_fin, g + 1)
                if below(g, GROUPS - 1):
                    sp.dma_start(out[bass.ds(g * W, W), :].rearrange("(j p) d -> p j d", p=P),
                                 out_o[:, slot, :].rearrange("p (j d) -> p j d", j=4)).then_inc(s_out[slot], 16)
                else:
                    t, p = divmod(NEW - LAST, P)
                    end = LAST + (t + 1) * P
                    sp.dma_start(out[NEW:end, :], out_o[p:P, slot, t * D:(t + 1) * D]).then_inc(s_out[slot], 16)
                    sp.dma_start(out[end:N, :].rearrange("(j p) d -> p j d", p=P),
                                 out_o[:, slot, (t + 1) * D:].rearrange("p (j d) -> p j d", j=3 - t)
                                 ).then_inc(s_out[slot], 16)

            def body(g, slot, use):
                if below(g, GROUPS):
                    if at_least(g, 4):
                        sp.wait_ge(s_fin, g - 3)
                    sp.dma_start(hu_i[:, slot, :], hu_d[g]).then_inc(s_ld[slot], 16)
                    sp.dma_start(xh_i[:, slot, :], xh_d[g]).then_inc(s_ld[slot], 16)
                if at_least(g, 4):
                    store(g - 4, slot, use - 1)

            run_steps(sp, GROUPS + 4, 4, GROUPS, 4, body)
            for slot in range(4):
                uses = len(range(slot, GROUPS, 4)) + (slot == (GROUPS - 1) % 4)
                sp.wait_ge(s_out[slot], 16 * uses)

        def gpsimd_2(pool):
            pool.memset(hop[:], float(W)).then_inc(s_hop, 1)
            pool.wait_ge(s_hop, 1)
            pool.iota(ids[:, 0, :], [[1, W]], base=0, channel_multiplier=0,
                      allow_small_or_imprecise_dtypes=True).then_inc(s_ids, 1)

            def body(g, slot, use):
                if below(g, GROUPS - 1):
                    pool.wait_ge(s_ids, g + 1)
                    if at_least(g, 1):
                        pool.wait_ge(s_a, 4 * g)
                        pool.wait_ge(s_un, g)
                    to, of = ids[:, (slot + 1) % 2, :], ids[:, slot % 2, :]
                    if below(g, GROUPS - 2):
                        pool.tensor_tensor(to, of, hop, ALU.add).then_inc(s_ids, 1)
                    else:
                        pool.tensor_scalar(to, of, float(LAST - (GROUPS - 2) * W), None, ALU.add).then_inc(s_ids, 1)
                pool.wait_ge(s_ld[slot], 32 * use + 32)
                pool.tensor_tensor(xh_i[:, slot, :], xh_i[:, slot, :], b_out[:], ALU.add).then_inc(s_xb, 1)

            run_steps(pool, GROUPS, 1, GROUPS - 2, 4, body)

        def load_ranges(eng, regs, g):
            eng.load(regs, ranges[0:1, bass.ds(g * 8, 8)])
            return [(eng.snap(regs[2 * j], min_val=0, max_val=ET - 1),
                     eng.snap(regs[2 * j + 1], min_val=1, max_val=ET)) for j in range(4)]

        def vector_2(dve):
            regs = [dve.alloc_register(f"dve_range{i}") for i in range(8)]
            made = [dve.alloc_register(f"dve_made{j}") for j in range(4)]
            for r in made:
                dve.reg_mov(r, 0)

            def onehots(g, slot, use):
                par = slot % 2
                ranges_of = load_ranges(dve, regs, g)
                dve.wait_ge(s_ids, g + 1)
                if at_least(g, 2):
                    dve.wait_ge(s_t2, g - 1)
                for j, (lo, hi) in enumerate(ranges_of):
                    node = ids[:, par, j * P:(j + 1) * P]

                    def onehot(to, k):
                        return dve.tensor_scalar(to, node, dst_f[:, bass.ds(k, 1)], None, ALU.is_equal)

                    def another(k):
                        onehot(hot_b[:, par, j, :], k).then_inc(s_b[j], 1)
                        dve.reg_add(made[j], made[j], 1)

                    onehot(hot_a[:, par, j, :], lo).then_inc(s_a, 1)
                    with dve.If(hi > lo + 1):
                        another(lo + 1)
                    with dve.If(hi > lo + 2):
                        with dve.Fori(lo + 2, hi) as k:
                            dve.wait_ge(s_bu[j], dve.snap(made[j], min_val=0, max_val=GROUPS * ET))
                            another(k)

            def add_hu(g, slot, use):
                dve.wait_ge(s_t2, g + 1)
                dve.wait_ge(s_ld[slot], 32 * use + 32)
                dve.tensor_tensor(u_n[:, slot % 2, :], p_agg[slot % 2][:], hu_i[:, slot, :], ALU.add).then_inc(s_un, 1)

            def finish(g, slot, use):
                dve.wait_ge(s_o, g + 1)
                dve.wait_ge(s_xb, g + 1)
                if at_least(g, 4):
                    dve.wait_ge(s_out[slot], 16 * use)
                dve.tensor_tensor(out_o[:, slot, :], p_out[slot % 2][:], xh_i[:, slot, :], ALU.add).then_inc(s_fin, 1)

            def body(g, slot, use):
                if below(g, GROUPS):
                    onehots(g, slot, use)
                if at_least(g, 1) and below(g, GROUPS + 1):
                    add_hu(g - 1, (slot - 1) % 4, use - (slot < 1))
                if at_least(g, 3):
                    finish(g - 3, (slot - 3) % 4, use - (slot < 3))

            run_steps(dve, GROUPS + 3, 7, GROUPS, 4, body)

        def scalar_2(act):
            def body(g, slot, use):
                act.wait_ge(s_t2, g + 2)
                act.activation(u_t[:, slot, :], p_ut[slot][:], ACT.Relu, bias=b_u1[:]).then_inc(s_ut, 1)

            run_steps(act, GROUPS, 0, GROUPS, 2, body)

        def tensor_2(pe):
            regs = [pe.alloc_register(f"pe_range{i}") for i in range(8)]
            used = [pe.alloc_register(f"pe_used{j}") for j in range(4)]
            for r in used:
                pe.reg_mov(r, 0)

            def sums(g, slot, use):
                par = slot % 2
                ranges_of = load_ranges(pe, regs, g)
                if at_least(g, 2):
                    pe.wait_ge(s_un, g - 1)
                for j, (lo, hi) in enumerate(ranges_of):
                    to = p_agg[par][:, j * D:(j + 1) * D]

                    def another(k):
                        pe.reg_add(used[j], used[j], 1)
                        pe.wait_ge(s_b[j], pe.snap(used[j], min_val=0, max_val=GROUPS * ET))
                        pe.matmul(to, hot_b[:, par, j, :], msgs[:, k, :], start=False, stop=True,
                                  skip_group_check=True).then_inc(s_bu[j], 1)

                    pe.wait_ge(s_a, 4 * g + j + 1)
                    pe.matmul(to, hot_a[:, par, j, :], msgs[:, lo, :], start=True, stop=True, skip_group_check=True)
                    with pe.If(hi > lo + 1):
                        another(lo + 1)
                    with pe.If(hi > lo + 2):
                        with pe.Fori(lo + 2, hi) as k:
                            another(k)

            def transposes(g, slot):
                for j in range(4):
                    if slot is None:
                        ins = pe.transpose(p_ut[1][:, j * P:(j + 1) * P], ident[:], ident[:])
                    else:
                        ins = pe.transpose(p_ut[slot][:, j * P:(j + 1) * P], u_n[:, slot, j * P:(j + 1) * P], ident[:])
                ins.then_inc(s_t2, 1)

            def body(g, slot, use):
                if below(g, GROUPS):
                    sums(g, slot, use)
                if not at_least(g, 1):
                    transposes(None, None)
                elif below(g, GROUPS + 1):
                    pe.wait_ge(s_un, g)
                    if at_least(g, 3):
                        pe.wait_ge(s_ut, g - 2)
                    transposes(g - 1, (slot - 1) % 2)
                if at_least(g, 2):
                    pe.wait_ge(s_ut, g - 1)
                    if at_least(g, 4):
                        pe.wait_ge(s_fin, g - 3)
                    for j in range(4):
                        ins = pe.matmul(p_out[slot % 2][:, j * D:(j + 1) * D], u_t[:, slot % 2, j * P:(j + 1) * P],
                                        w_out[:], start=True, stop=True)
                    ins.then_inc(s_o, 1)

            run_steps(pe, GROUPS + 2, 4, GROUPS, 2, body)

        with nc.Block() as block:
            block.sync(sync_2)
            block.gpsimd(gpsimd_2)
            block.vector(vector_2)
            block.scalar(scalar_2)
            block.tensor(tensor_2)


def kernel(**inputs):
    import concourse.bacc as bacc
    from concourse.bass_utils import run_bass_kernel_spmd

    src = np.asarray(inputs["src"]).astype(np.int32)
    dst = np.asarray(inputs["dst"]).astype(np.int32)
    pad = ET * P - E
    both = np.stack([np.pad(a, (0, pad)).reshape(STEPS, 4, P) for a in (src, dst)], 1)
    ends = np.ascontiguousarray(both.reshape(STEPS, 8, P).transpose(2, 0, 1))
    dst_rows = np.pad(dst, (0, pad), mode="edge").reshape(ET // 2, 2, P)
    dst_cols = np.pad(dst, (0, pad + P), constant_values=-1).reshape(ET + 1, P).T
    edge_t = np.pad(np.asarray(inputs["edge_attr_32"]), ((0, pad), (0, 0))).T

    def get(name):
        return np.asarray(inputs["L0_gnn_" + name])

    arrays = {
        "x": np.asarray(inputs["x"]), "ends": ends, "dst_rows": dst_rows, "dst_cols": dst_cols, "edge_t": edge_t,
        "wm1": get("Wm1"), "bm1": get("bm1").reshape(D, 1), "wm2": get("Wm2"), "bm2": get("bm2").reshape(D, 1),
        "wu1": get("Wu1"), "bu1": get("bu1").reshape(D, 1), "wu2": get("Wu2"),
        "bu2": np.broadcast_to(get("bu2"), (P, 4, D)).reshape(P, W),
    }
    arrays = {k + "_in": np.ascontiguousarray(v) for k, v in arrays.items()}
    nc = bacc.Bacc("TRN2", target_bir_lowering=False, num_devices=1)
    args = [nc.dram_tensor(k, v.shape, mybir.dt.from_np(v.dtype), kind="ExternalInput").ap() for k, v in arrays.items()]
    out = nc.dram_tensor("out", (N, D), F32, kind="ExternalOutput").ap()
    build(nc, *args, out)
    return run_bass_kernel_spmd(nc, [arrays], core_ids=[0]).results[0]["out"]
```

```python
from contextlib import ExitStack

import numpy as np

import concourse.bass as bass
from concourse import mybir

F32 = mybir.dt.float32
F32R = mybir.dt.float32r
I32 = mybir.dt.int32
ALU = mybir.AluOpType
ACT = mybir.ActivationFunctionType
AX_X = mybir.AxisListType.X

P = 128
N, E, D, DE = 50000, 25000, 128, 32
W = 4 * P
STEPS = -(-E // W)
ET = 4 * STEPS
SPARE = 3
GROUPS = -(-N // W)
LAST = N - W
NEW = (GROUPS - 1) * W
EPS = 1e-5
STAT = 12
TABLE = 18
assert GROUPS == 2 * STEPS


def run_steps(eng, total, first, last, unroll, body):
    first, last = -(-first // unroll) * unroll, last // unroll * unroll
    for s in range(first):
        body(s, s % unroll, s // unroll)
    with eng.Fori(first // unroll, last // unroll) as use:
        for slot in range(unroll):
            body(use * unroll + slot, slot, use)
    for s in range(last, total):
        body(s, s % unroll, s // unroll)


def at_least(s, k):
    return not isinstance(s, int) or s >= k


def below(s, k):
    return not isinstance(s, int) or s < k


def build(nc, x, ends, dst_rows, dst_cols, edge_t, wm1, bm1, wm2, bm2, wu1, bu1, wu2, bu2, out):
    with ExitStack() as ctx:
        def sb(name, shape, dt=F32, on=ctx):
            return on.enter_context(nc.sbuf_tensor(name, shape, dt))

        def ps(name, shape, dt=F32):
            return ctx.enter_context(nc.psum_tensor(name, shape, dt))

        def sem(name):
            return ctx.enter_context(nc.semaphore(name))

        ht_d = nc.dram_tensor("ht_scratch", (GROUPS, P, W), F32).ap()
        xh_d = nc.dram_tensor("xh_scratch", (GROUPS, P, W), F32).ap()
        ext_d = nc.dram_tensor("extremes_scratch", (2, ET), F32).ap()
        rng_d = nc.dram_tensor("ranges_scratch", (GROUPS, 2), I32).ap()

        w_src, w_dst, w_msg = sb("w_src", [P, D]), sb("w_dst", [P, D]), sb("w_msg", [P, D])
        w_edge = sb("w_edge", [DE, D])
        w_uh, w_ua, w_out = sb("w_uh", [P, D]), sb("w_ua", [P, D]), sb("w_out", [P, D])
        b_m1, b_m2, b_u1 = sb("b_m1", [P, 1]), sb("b_m2", [P, 1]), sb("b_u1", [P, 1])
        b_out = sb("b_out", [P, W])
        dst_f = sb("dst_f", [P, ET + SPARE])
        node = sb("node", [P, W])
        minus_base = sb("minus_base", [P, GROUPS])
        ranges = sb("ranges", [1, GROUPS * 2], I32)
        msgs = sb("msgs", [P, ET + SPARE, D])
        banks = [ps(f"bank{i}", [P, W]) for i in range(8)]

        s_w = sem("weights_loaded")
        s_idx = sem("indices_loaded")
        s_cst = sem("constants_made")
        s_pre = sem("table_steps")
        s_ext = sem("extremes_moved")
        s_rng = sem("ranges_moved")
        s_xn = [sem(f"nodes_loaded{i}") for i in range(4)]
        s_xg = [sem(f"ends_gathered{i}") for i in range(4)]
        s_cp = sem("ends_copied")
        s_stat = sem("stat")
        s_sd = sem("sd_ready")
        s_zv = sem("z_by_vector")
        s_za = sem("z_by_scalar")
        s_xh = sem("xh_ready")
        s_tr = sem("transposed")
        s_ht = sem("ht_ready")
        s_m1, s_m2, s_msg = sem("m1_summed"), sem("m2_summed"), sem("msg_summed")
        s_m1t, s_m2t, s_msgs = sem("m1t_ready"), sem("m2t_ready"), sem("msgs_ready")
        s_sto = [sem(f"scratch_stored{i}") for i in range(2)]

        s_ldh = [sem(f"ht_loaded{i}") for i in range(4)]
        s_ldx = [sem(f"xh_loaded{i}") for i in range(4)]
        s_hot, s_hot_x = sem("onehots_ready"), sem("more_onehots_ready")
        s_hi, s_hi_x = sem("high_parts_ready"), sem("more_high_parts_ready")
        s_lo, s_lo_x = sem("low_parts_ready"), sem("more_low_parts_ready")
        s_used = [sem(f"further_tiles_used{i}") for i in range(2)]
        s_agg = sem("u_summed")
        s_ut = sem("u_ready")
        s_xb = sem("xh_biased")
        s_o = sem("out_summed")
        s_fin = sem("out_ready")
        s_out = [sem(f"out_stored{i}") for i in range(4)]

        with ExitStack() as one:
            ident = sb("ident", [P, P], on=one)
            ends_all = sb("ends_all", [P, STEPS, 8], I32, on=one)
            ends_now = sb("ends_now", [P, 4, 8], I32, on=one)
            dst_i = sb("dst_i", [P, ET + SPARE], I32, on=one)
            node_i = sb("node_i", [P, W], I32, on=one)
            minus_i = sb("minus_i", [P, GROUPS], I32, on=one)
            rows_i = sb("rows_i", [ET // 2, 2, P], I32, on=one)
            ext = sb("ext", [ET // 2, 2, 2], on=one)
            base_i = sb("base_i", [GROUPS, 1], I32, on=one)
            up_i, down_i = sb("up_i", [P, ET], I32, on=one), sb("down_i", [P, ET], I32, on=one)
            first, last = sb("first", [GROUPS, 1], on=one), sb("last", [GROUPS, 1], on=one)
            lo_f, hi_f = sb("lo_f", [GROUPS, 1], on=one), sb("hi_f", [GROUPS, 1], on=one)
            rng_i = sb("rng_i", [GROUPS, 2], I32, on=one)

            xg = sb("xg", [P, 4, 8, D], on=one)
            xn = sb("xn", [P, 4, 8, D], on=one)
            zn = sb("zn", [P, 2, 8, D], on=one)
            edge = sb("edge", [DE, 4, W], on=one)
            bn = sb("bn", [P, 2, 16, 6], on=one)
            pair, diff = sb("pair", [P, 16, 2], on=one), sb("diff", [P, 16], on=one)
            sq, var, sd = (sb(n, [P, 16], on=one) for n in ("sq", "var", "sd"))
            veps, r0, r1, r2 = (sb(n, [P, 16], on=one) for n in ("veps", "r0", "r1", "r2"))
            mean, rstd, shift = (sb(n, [P, 2, 16], on=one) for n in ("mean", "rstd", "shift"))
            ht = sb("ht", [P, 2, 4, W], on=one)
            m1t, m2t = sb("m1t", [P, W], on=one), sb("m2t", [P, W], on=one)
            xh_o = sb("xh_o", [P, 2, 2, W], on=one)

            spare = zn[:, 0, :, :].rearrange("p t d -> p (t d)")
            ext_all = spare[:, 0:2 * ET].rearrange("p (a k) -> p a k", a=2)
            up_f, down_f = spare[:, 2 * ET:3 * ET], spare[:, 3 * ET:4 * ET]
            spare = zn[:, 1, :, :].rearrange("p t d -> p (t d)")[0:GROUPS]
            reaches, hit = spare[:, 0:ET], spare[:, ET:2 * ET]
            ahead, behind = spare[:, 2 * ET:3 * ET], spare[:, 3 * ET:4 * ET]
            rows_f = xh_o[0:ET // 2, 0, 0, 0:2 * P].rearrange("q (k e) -> q k e", k=2)

            p_tr, (p_m1, p_m2, p_msg) = banks[0:4], banks[4:7]

            def sync_1(sp):
                sp.dma_start(ends_all[:], ends).then_inc(s_idx, 16)
                sp.dma_start(rows_i[:], dst_rows).then_inc(s_ext, 16)

                def load_nodes(s, slot):
                    if below(s, STEPS - 1):
                        sp.dma_start(xn[:, slot], x[bass.ds(s * 2 * W, 2 * W), :].rearrange("(j p) d -> p j d", p=P)
                                     ).then_inc(s_xn[slot], 16)
                    else:
                        for h, row in enumerate((s * 2 * W, LAST)):
                            sp.dma_start(xn[:, slot, 4 * h:4 * h + 4],
                                         x[row:row + W, :].rearrange("(j p) d -> p j d", p=P)).then_inc(s_xn[slot], 16)
                    sp.dma_start(edge[:, slot], edge_t[:, bass.ds(s * W, W)]).then_inc(s_xn[slot], 16)

                load_nodes(0, 0)
                sp.dma_start(dst_i[:], dst_cols).then_inc(s_ext, 16)
                sp.dma_start(b_m1[:], bm1).then_inc(s_w, 16)
                sp.dma_start(b_m2[:], bm2).then_inc(s_w, 16)
                sp.dma_start(b_u1[:], bu1).then_inc(s_w, 16)
                sp.wait_ge(s_pre, 3)
                for a in range(2):
                    sp.dma_start(ext_d[a].rearrange("(q k) -> q k", k=2), ext[:, a, :]).then_inc(s_ext, 16)
                load_nodes(1, 1)
                sp.wait_ge(s_ext, 64)
                for a in range(2):
                    sp.dma_start(ext_all[:, a, :], ext_d[a].partition_broadcast(P)).then_inc(s_ext, 16)
                for to, of in ((w_src, wm1[0:D]), (w_dst, wm1[D:2 * D]), (w_edge, wm1[2 * D:2 * D + DE]), (w_msg, wm2),
                               (w_ua, wu1[D:2 * D])):
                    sp.dma_start(to[:], of).then_inc(s_w, 16)
                load_nodes(2, 2)
                load_nodes(3, 3)
                for to, of in ((w_uh, wu1[0:D]), (w_out, wu2), (b_out, bu2)):
                    sp.dma_start(to[:], of).then_inc(s_w, 16)
                sp.wait_ge(s_pre, TABLE)
                sp.dma_start(rng_d, rng_i[:]).then_inc(s_rng, 16)
                sp.wait_ge(s_rng, 16)
                sp.dma_start(ranges[:], rng_d.rearrange("(o g) c -> o (g c)", o=1)).then_inc(s_rng, 16)

                def body(s, slot, use):
                    if below(s, STEPS) and at_least(s, 4):
                        sp.wait_ge(s_xh, 2 * (s - 3))
                        sp.wait_ge(s_m1, s - 3)
                        load_nodes(s, slot)
                    if at_least(s, 3):
                        to, half = bass.ds(2 * (s - 3), 2), (slot + 1) % 2
                        sp.wait_ge(s_ht, 4 * (s - 2))
                        sp.dma_start(ht_d[to].rearrange("g p f -> p g f"), ht[:, half, 2:4]).then_inc(s_sto[half], 16)
                        sp.wait_ge(s_xh, 2 * (s - 2))
                        sp.dma_start(xh_d[to].rearrange("g p f -> p g f"), xh_o[:, half]).then_inc(s_sto[half], 16)

                run_steps(sp, STEPS + 3, 4, STEPS - 1, 4, body)
                sp.wait_ge(s_rng, 32)
                for half in range(2):
                    sp.wait_ge(s_sto[half], 32 * ((STEPS + 1 - half) // 2))

            def gpsimd_1(pool):
                pool.iota(base_i[:], [[0, 1]], base=0, channel_multiplier=W).then_inc(s_cst, 1)
                pool.iota(up_i[:], [[1, ET]], base=1, channel_multiplier=0).then_inc(s_cst, 1)
                pool.iota(down_i[:], [[-1, ET]], base=ET, channel_multiplier=0).then_inc(s_cst, 1)
                pool.iota(node_i[:], [[1, W]], base=0, channel_multiplier=0).then_inc(s_cst, 1)
                pool.iota(minus_i[:], [[-W, GROUPS]], base=0, channel_multiplier=0).then_inc(s_cst, 1)
                pool.memset(ident[:], 0.0).then_inc(s_cst, 1)
                pool.memset(msgs[:, ET:, :], 0.0).then_inc(s_cst, 1)
                pool.wait_ge(s_idx, 16)
                pool.tensor_copy(ends_now[:, 0], ends_all[:, 0, :]).then_inc(s_cp, 1)

                def body(s, slot, use):
                    pool.wait_ge(s_cp, s + 1)
                    if at_least(s, 4):
                        pool.wait_ge(s_tr, 4 * (s - 3) - 2)
                    if below(s, STEPS - 1):
                        if at_least(s, 3):
                            pool.wait_ge(s_xg[(slot + 1) % 4], 128 * use + (128 if slot == 3 else 0))
                        pool.tensor_copy(ends_now[:, (slot + 1) % 4], ends_all[:, s + 1, :]).then_inc(s_cp, 1)
                    for t in range(8):
                        pool.indirect_dma_start(
                            xg[:, slot, t, :], None, x,
                            bass.IndirectOffsetOnAxis(ap=ends_now[:, slot, t:t + 1], axis=0)).then_inc(s_xg[slot], 16)
                    if not at_least(s, 1):
                        pool.wait_ge(s_cst, 6)
                        pool.affine_select(out=ident[:], in_=ident[:], compare_op=ALU.not_equal, fill=1.0, base=0,
                                           pattern=[[-1, P]], channel_multiplier=1).then_inc(s_cst, 1)

                run_steps(pool, STEPS, 4, STEPS - 1, 4, body)

            def start_table(dve, did):
                dve.wait_ge(s_ext, 32)
                did(dve.tensor_copy(rows_f, rows_i[:]))
                did(dve.tensor_reduce(ext[:, 0, :], rows_f, AX_X, ALU.min), False)
                did(dve.tensor_reduce(ext[:, 1, :], rows_f, AX_X, ALU.max), False)
                did(dve.tensor_copy(dst_f[:], dst_i[:]), False)
                dve.wait_ge(s_cst, 5)
                did(dve.tensor_copy(node[:], node_i[:]), False)
                did(dve.tensor_copy(minus_base[:], minus_i[:]), False)
                did(dve.tensor_copy(up_f, up_i[:]), False)
                did(dve.tensor_copy(down_f, down_i[:]))
                did(dve.memset(minus_base[:, GROUPS - 1:GROUPS], -float(LAST)), False)
                did(dve.tensor_scalar(first[:], base_i[:], float(LAST), None, ALU.min), False)
                did(dve.tensor_scalar(last[:], base_i[:], float(LAST), float(W - 1), ALU.min, ALU.add))

            def finish_table(dve, did):
                dve.wait_ge(s_ext, 96)
                did(dve.tensor_scalar(reaches, ext_all[0:GROUPS, 1, :], first[:], None, ALU.is_ge))
                did(dve.scalar_tensor_tensor(out=hit, in0=ext_all[0:GROUPS, 0, :], scalar=last[:],
                                             in1=reaches, op0=ALU.is_le, op1=ALU.mult))
                dve.tensor_tensor(ahead, hit, up_f[0:GROUPS], ALU.mult)
                did(dve.tensor_tensor(behind, hit, down_f[0:GROUPS], ALU.mult))
                dve.tensor_reduce(hi_f[:], ahead, AX_X, ALU.max)
                did(dve.tensor_reduce(lo_f[:], behind, AX_X, ALU.max))
                did(dve.tensor_scalar(r0[0:GROUPS, 0:1], lo_f[:], 2.0, None, ALU.max))
                dve.tensor_scalar(rng_i[:, 0:1], r0[0:GROUPS, 0:1], -1.0, float(ET), ALU.mult, ALU.add)
                did(dve.tensor_scalar(r1[0:GROUPS, 0:1], r0[0:GROUPS, 0:1], -1.0, float(ET + 2), ALU.mult, ALU.add))
                did(dve.tensor_tensor(rng_i[:, 1:2], r1[0:GROUPS, 0:1], hi_f[:], ALU.max))

            VECTOR_TILES = 9

            def vector_1(dve):
                steps = [0]

                def did(ins, wait=True):
                    steps[0] += 1
                    ins.then_inc(s_pre, 1)
                    if wait:
                        dve.wait_ge(s_pre, steps[0])

                start_table(dve, did)

                def stat_of_nodes(s, slot, t):
                    dve.bn_stats(bn[:, slot % 2, 8 + t, :], xn[:, slot, t, :])

                def stat_of_ends(s, slot, use):
                    dve.wait_ge(s_xg[slot], 128 * use + 128)
                    for t in range(8):
                        ins = dve.bn_stats(bn[:, slot % 2, t, :], xg[:, slot, t, :])
                    ins.then_inc(s_stat, 1)

                def statistics(s, slot, between):
                    half = slot % 2
                    if at_least(s, 2):
                        dve.wait_ge(s_za, 2 * (s - 1))
                        dve.wait_ge(s_zv, 3 * (s - 1))
                    dve.wait_ge(s_stat, STAT * s + 1)
                    dve.tensor_tensor(pair[:], bn[:, half, :, 1:3], bn[:, half, :, 4:6], ALU.add).then_inc(s_stat, 1)
                    dve.tensor_tensor(diff[:], bn[:, half, :, 1], bn[:, half, :, 4], ALU.subtract).then_inc(s_stat, 1)
                    between(0)
                    dve.wait_ge(s_stat, STAT * s + 3)
                    dve.scalar_tensor_tensor(out=sq[:], in0=diff[:], scalar=0.25, in1=diff[:], op0=ALU.mult,
                                             op1=ALU.mult).then_inc(s_stat, 1)
                    dve.tensor_scalar(mean[:, half], pair[:, :, 0], 0.5, None, ALU.mult).then_inc(s_stat, 1)
                    between(1)
                    dve.wait_ge(s_stat, STAT * s + 5)
                    dve.scalar_tensor_tensor(out=var[:], in0=pair[:, :, 1], scalar=1.0 / D, in1=sq[:], op0=ALU.mult,
                                             op1=ALU.add).then_inc(s_stat, 1)
                    between(2)
                    dve.wait_ge(s_stat, STAT * s + 6)
                    dve.tensor_scalar(veps[:], var[:], EPS, None, ALU.add).then_inc(s_stat, 1)
                    for i in range(3, 6):
                        between(i)
                    dve.wait_ge(s_sd, s + 1)
                    dve.reciprocal(r0[:], sd[:]).then_inc(s_stat, 1)
                    between(6)
                    dve.wait_ge(s_stat, STAT * s + 8)
                    dve.scalar_tensor_tensor(out=r1[:], in0=r0[:], scalar=-0.5, in1=r0[:], op0=ALU.mult,
                                             op1=ALU.mult).then_inc(s_stat, 1)
                    between(7)
                    dve.wait_ge(s_stat, STAT * s + 9)
                    dve.tensor_tensor(r2[:], r1[:], veps[:], ALU.mult).then_inc(s_stat, 1)
                    between(8)
                    dve.wait_ge(s_stat, STAT * s + 10)
                    dve.scalar_tensor_tensor(out=rstd[:, half], in0=r2[:], scalar=1.5, in1=r0[:], op0=ALU.add,
                                             op1=ALU.mult).then_inc(s_stat, 1)
                    between(9)
                    dve.wait_ge(s_stat, STAT * s + 11)
                    dve.scalar_tensor_tensor(out=shift[:, half], in0=mean[:, half], scalar=-1.0, in1=rstd[:, half], op0=ALU.mult,
                                             op1=ALU.mult).then_inc(s_stat, 1)

                def x_plus_h(s, slot, h):
                    half = slot % 2
                    dve.scalar_tensor_tensor(
                        out=xh_o[:, half, h, :].rearrange("p (j d) -> p j d", j=4), in0=zn[:, half, 4 * h:4 * h + 4, :],
                        scalar=0.0, in1=xn[:, slot, 4 * h:4 * h + 4, :], op0=ALU.max, op1=ALU.add).then_inc(s_xh, 1)

                def normalise(s, slot):
                    if at_least(s, 2):
                        dve.wait_ge(s_tr, 4 * (s - 1))
                        dve.wait_ge(s_xh, 2 * (s - 1))
                    for t in range(VECTOR_TILES):
                        if t < 8:
                            of = to = xg[:, slot, t, :]
                        else:
                            of, to = xn[:, slot, t - 8, :], zn[:, slot % 2, t - 8, :]
                        ins = dve.tensor_scalar(to, of, mean[:, slot % 2, t:t + 1], rstd[:, slot % 2, t:t + 1],
                                                ALU.subtract, ALU.mult)
                        if t in (3, 7, VECTOR_TILES - 1):
                            ins.then_inc(s_zv, 1)

                def body(s, slot, use):
                    prev, prev2 = (slot - 1) % 4, (slot - 2) % 4
                    if below(s, STEPS):
                        dve.wait_ge(s_xn[slot], 32 * use + 32 + (0 if below(s, STEPS - 1) else 16))
                    def between(i):
                        if i < 8 and below(s, STEPS):
                            stat_of_nodes(s, slot, i)
                        if i == 8 and at_least(s, 2):
                            dve.wait_ge(s_za, 2 * (s - 1))
                            dve.wait_ge(s_zv, 3 * (s - 1))
                            if at_least(s, 4):
                                dve.wait_ge(s_sto[slot % 2], 64 * use + (32 if slot >= 2 else 0) - 32)
                        if i >= 8 and at_least(s, 2):
                            x_plus_h(s - 2, prev2, i - 8)

                    if at_least(s, 1) and below(s, STEPS + 1):
                        statistics(s - 1, prev, between)
                        normalise(s - 1, prev)
                    else:
                        for i in range(10):
                            between(i)
                    if not at_least(s, 1):
                        finish_table(dve, did)
                        assert steps[0] == TABLE
                    if below(s, STEPS):
                        stat_of_ends(s, slot, use)

                run_steps(dve, STEPS + 2, 4, STEPS - 1, 4, body)

            def scalar_1(act):
                act.wait_ge(s_w, 16 * 11)

                def body(s, slot, use):
                    has_norm, has_msg = at_least(s, 1) and below(s, STEPS + 1), at_least(s, 2)
                    prev = (slot - 1) % 4

                    def normalise(tiles):
                        for t in tiles:
                            ins = act.activation(zn[:, prev % 2, t - 8, :], xn[:, prev, t - 8, :], ACT.Identity,
                                                 bias=shift[:, prev % 2, t:t + 1], scale=rstd[:, prev % 2, t:t + 1])
                        ins.then_inc(s_za, 1)

                    def relu(qs):
                        for q in qs:
                            act.wait_ge(s_tr, 4 * (s - 1) + q + 1)
                            act.activation(ht[:, prev % 2, q, :], p_tr[q][:], ACT.Relu).then_inc(s_ht, 1)

                    if has_norm:
                        act.wait_ge(s_stat, STAT * (s - 1) + 7)
                        act.activation(sd[:], veps[:], ACT.Sqrt).then_inc(s_sd, 1)
                    if has_msg:
                        act.wait_ge(s_m1, s - 1)
                        act.activation(m1t[:], p_m1[:], ACT.Relu, bias=b_m1[:]).then_inc(s_m1t, 1)
                    if has_norm:
                        act.wait_ge(s_stat, STAT * (s - 1) + 12)
                        normalise(range(VECTOR_TILES, 12))
                    if has_msg:
                        act.wait_ge(s_m2, s - 1)
                        act.activation(m2t[:], p_m2[:], ACT.Relu, bias=b_m2[:]).then_inc(s_m2t, 1)
                    if has_norm:
                        normalise(range(12, 16))
                    if has_norm:
                        if at_least(s, 3):
                            act.wait_ge(s_sto[prev % 2], 64 * use + (-32, 0, 0, 32)[slot])
                        relu(range(2))
                    if has_msg:
                        act.wait_ge(s_msg, s - 1)
                        act.activation(msgs[:, bass.ds(4 * (s - 2), 4), :], p_msg[:].rearrange("p (j d) -> p j d", j=4),
                                       ACT.Copy).then_inc(s_msgs, 1)
                    if has_norm:
                        relu(range(2, 4))

                run_steps(act, STEPS + 2, 4, STEPS - 1, 4, body)

            def tensor_1(pe):
                pe.wait_ge(s_w, 16 * 11)
                pe.wait_ge(s_cst, 8)

                def transposes(s, slot, qs):
                    for q in qs:
                        pe.wait_ge(s_zv, 3 * s + min(q, 2) + 1)
                        if q >= 2:
                            pe.wait_ge(s_za, 2 * s + q - 1)
                        if at_least(s, 1):
                            pe.wait_ge(s_ht, 4 * (s - 1) + q + 1)
                        for j in range(4):
                            of = xg[:, slot, 4 * q + j, :] if q < 2 else zn[:, slot % 2, 4 * (q - 2) + j, :]
                            ins = pe.transpose(p_tr[q][:, j * P:(j + 1) * P], of, ident[:])
                        ins.then_inc(s_tr, 1)

                def messages(s, slot, use, part):
                    if part == 0:
                        pe.wait_ge(s_ht, 4 * s + 2)
                        pe.wait_ge(s_xn[slot], 32 * use + 32 + (0 if below(s, STEPS - 1) else 16))
                        if at_least(s, 1):
                            pe.wait_ge(s_m1t, s)
                        pe.matmul(p_m1[:], w_src[:], ht[:, slot % 2, 0, :], start=True, stop=False)
                        pe.matmul(p_m1[:], w_dst[:], ht[:, slot % 2, 1, :], start=False, stop=False)
                        pe.matmul(p_m1[:], w_edge[:], edge[:, slot, :], start=False, stop=True).then_inc(s_m1, 1)
                    if part == 1:
                        pe.wait_ge(s_m1t, s + 1)
                        pe.matmul(p_m2[:], w_msg[:], m1t[:], start=True, stop=True).then_inc(s_m2, 1)
                    if part == 2:
                        pe.wait_ge(s_m2t, s + 1)
                        if at_least(s, 1):
                            pe.wait_ge(s_msgs, s)
                        for j in range(4):
                            ins = pe.matmul(p_msg[:, j * D:(j + 1) * D], m2t[:, j * P:(j + 1) * P], w_ua[:],
                                            start=True, stop=True)
                        ins.then_inc(s_msg, 1)

                def body(s, slot, use):
                    prev, prev2 = (slot - 1) % 4, (slot - 2) % 4
                    for part, qs in enumerate(((), (0, 1), (2, 3))):
                        if at_least(s, 2):
                            messages(s - 2, prev2, use - (slot < 2), part)
                        if at_least(s, 1) and below(s, STEPS + 1):
                            transposes(s - 1, prev, qs)

                run_steps(pe, STEPS + 2, 4, STEPS - 1, 4, body)

            with nc.Block() as block:
                block.sync(sync_1)
                block.gpsimd(gpsimd_1)
                block.vector(vector_1)
                block.scalar(scalar_1)
                block.tensor(tensor_1)

        with ExitStack() as two:
            hot = sb("hot", [P, 10, W], F32R, on=two)
            high, low = sb("high", [P, 10, D], F32R, on=two), sb("low", [P, 10, D], F32R, on=two)
            ht_i, xh_i = sb("ht_i", [P, 4, W], on=two), sb("xh_i", [P, 4, W], on=two)
            u_t = sb("u_t", [P, 2, W], on=two)
            out_o = sb("out_o", [P, 4, W], on=two)
            p_agg, p_out = banks[0:2], banks[2:4]

            def sync_2(sp):
                def store(g, slot):
                    sp.wait_ge(s_fin, g + 1)
                    if below(g, GROUPS - 1):
                        sp.dma_start(out[bass.ds(g * W, W), :].rearrange("(j p) d -> p j d", p=P),
                                     out_o[:, slot, :].rearrange("p (j d) -> p j d", j=4)).then_inc(s_out[slot], 16)
                    else:
                        t, p = divmod(NEW - LAST, P)
                        end = LAST + (t + 1) * P
                        sp.dma_start(out[NEW:end, :], out_o[p:P, slot, t * D:(t + 1) * D]).then_inc(s_out[slot], 16)
                        sp.dma_start(out[end:N, :].rearrange("(j p) d -> p j d", p=P),
                                     out_o[:, slot, (t + 1) * D:].rearrange("p (j d) -> p j d", j=3 - t)
                                     ).then_inc(s_out[slot], 16)

                def body(g, slot, use):
                    if below(g, GROUPS):
                        if at_least(g, 4):
                            sp.wait_ge(s_fin, g - 3)
                        sp.dma_start(ht_i[:, slot, :], ht_d[g]).then_inc(s_ldh[slot], 16)
                        sp.dma_start(xh_i[:, slot, :], xh_d[g]).then_inc(s_ldx[slot], 16)
                    if at_least(g, 4):
                        store(g - 4, slot)

                run_steps(sp, GROUPS + 4, 4, GROUPS, 4, body)
                for slot in range(4):
                    uses = len(range(slot, GROUPS, 4)) + (slot == (GROUPS - 1) % 4)
                    sp.wait_ge(s_out[slot], 16 * uses)

            class EdgeTiles:

                def __init__(self, eng, name):
                    self.eng = eng
                    self.regs = [eng.alloc_register(f"{name}_range{i}") for i in range(2)]
                    self.count = eng.alloc_register(f"{name}_count")
                    eng.reg_mov(self.count, 0)
                    self.in_pair = [eng.alloc_register(f"{name}_in_pair{i}") for i in range(2)]
                    for count in self.in_pair:
                        eng.reg_mov(count, 1)

                def up_to(self):
                    self.eng.reg_add(self.count, self.count, 1)
                    return self.eng.snap(self.count, min_val=1, max_val=GROUPS * ET)

                def wait_for_slot(self, pair):
                    count = self.in_pair[pair]
                    self.eng.wait_ge(s_used[pair], self.eng.snap(count, min_val=1, max_val=GROUPS * ET))
                    self.eng.reg_add(count, count, 1)

                def visit(self, g, par, regular, more):
                    eng = self.eng
                    eng.load(self.regs, ranges[0:1, bass.ds(g * 2, 2)])
                    lo = eng.snap(self.regs[0], min_val=0, max_val=ET - 2)
                    hi = eng.snap(self.regs[1], min_val=2, max_val=ET)
                    regular(lo, 2 * par, 0)
                    with eng.If(hi > lo + 2):
                        more(lo + 2, 4 + par, None)
                    with eng.If(hi > lo + 3):
                        with eng.Fori(lo + 3, hi, 4) as k:
                            more(k, 6, 0)
                            more(k + 1, 7, 0)
                            with eng.If(hi > k + 2):
                                more(k + 2, 8, 1)
                                more(k + 3, 9, 1)
                    regular(lo + 1, 2 * par + 1, 1)

            def gpsimd_2(pool):
                tiles = EdgeTiles(pool, "pool")

                def body(g, slot, use):
                    def part(k, at):
                        return pool.tensor_tensor(low[:, at, :], msgs[:, k, :], high[:, at, :].bitcast(F32), ALU.subtract)

                    def regular(k, at, n):
                        pool.wait_ge(s_hi, 2 * g + n + 1)
                        part(k, at).then_inc(s_lo, 1)

                    def more(k, at, pair):
                        pool.wait_ge(s_hi_x, tiles.up_to())
                        part(k, at).then_inc(s_lo_x, 1)

                    tiles.visit(g, slot % 2, regular, more)
                    pool.wait_ge(s_ldx[slot], 16 * use + 16)
                    pool.tensor_tensor(xh_i[:, slot, :], xh_i[:, slot, :], b_out[:], ALU.add).then_inc(s_xb, 1)

                run_steps(pool, GROUPS, 4, GROUPS, 4, body)

            def vector_2(dve):
                tiles = EdgeTiles(dve, "dve")

                def onehots(g, slot):
                    def onehot(k, at):
                        return dve.tensor_scalar(hot[:, at, :], node[:], dst_f[:, bass.ds(k, 1)],
                                                 minus_base[:, bass.ds(g, 1)], ALU.subtract, ALU.is_equal)

                    def regular(k, at, n):
                        onehot(k, at).then_inc(s_hot, 1)

                    def more(k, at, pair):
                        if pair is not None:
                            tiles.wait_for_slot(pair)
                        tiles.up_to()
                        onehot(k, at).then_inc(s_hot_x, 1)

                    if at_least(g, 2):
                        dve.wait_ge(s_agg, g - 1)
                    tiles.visit(g, slot % 2, regular, more)

                def finish(g, slot, use):
                    dve.wait_ge(s_o, g + 1)
                    dve.wait_ge(s_xb, g + 1)
                    if at_least(g, 4):
                        dve.wait_ge(s_out[slot], 16 * use)
                    dve.tensor_tensor(out_o[:, slot, :], p_out[slot % 2][:], xh_i[:, slot, :], ALU.add
                                      ).then_inc(s_fin, 1)

                def body(g, slot, use):
                    if below(g, GROUPS):
                        onehots(g, slot)
                    if at_least(g, 2):
                        finish(g - 2, (slot - 2) % 4, use - (slot < 2))

                run_steps(dve, GROUPS + 2, 6, GROUPS, 4, body)

            def scalar_2(act):
                tiles = EdgeTiles(act, "act")

                def high_parts(g, slot):
                    def part(k, at):
                        return act.activation(high[:, at, :], msgs[:, k, :], ACT.Copy)

                    def regular(k, at, n):
                        part(k, at).then_inc(s_hi, 1)

                    def more(k, at, pair):
                        if pair is not None:
                            tiles.wait_for_slot(pair)
                        tiles.up_to()
                        part(k, at).then_inc(s_hi_x, 1)

                    if at_least(g, 2):
                        act.wait_ge(s_agg, g - 1)
                    tiles.visit(g, slot % 2, regular, more)

                def body(g, slot, use):
                    if below(g, GROUPS):
                        high_parts(g, slot)
                    if at_least(g, 1):
                        act.wait_ge(s_agg, g)
                        if at_least(g, 3):
                            act.wait_ge(s_o, g - 2)
                        prev = (slot - 1) % 2
                        act.activation(u_t[:, prev, :], p_agg[prev][:], ACT.Relu, bias=b_u1[:]).then_inc(s_ut, 1)

                run_steps(act, GROUPS + 1, 4, GROUPS, 2, body)

            def tensor_2(pe):
                tiles = EdgeTiles(pe, "pe")
                for pair in range(2):
                    pe.matmul(p_out[0][:, 0:D], w_out[:], w_out[:], start=True, stop=True).then_inc(s_used[pair], 2)

                def sums(g, slot, use):
                    to = p_agg[slot % 2][:]

                    def add(at, stop):
                        pe.matmul(to, low[:, at, :], hot[:, at, :], start=False, stop=False, skip_group_check=True)
                        return pe.matmul(to, high[:, at, :], hot[:, at, :], start=False, stop=stop,
                                         skip_group_check=True)

                    def regular(k, at, n):
                        pe.wait_ge(s_hot, 2 * g + n + 1)
                        pe.wait_ge(s_lo, 2 * g + n + 1)
                        ins = add(at, n == 1)
                        if n == 1:
                            ins.then_inc(s_agg, 1)

                    def more(k, at, pair):
                        count = tiles.up_to()
                        pe.wait_ge(s_hot_x, count)
                        pe.wait_ge(s_lo_x, count)
                        ins = add(at, False)
                        if pair is not None:
                            ins.then_inc(s_used[pair], 1)

                    pe.wait_ge(s_ldh[slot], 16 * use + 16)
                    if at_least(g, 2):
                        pe.wait_ge(s_ut, g - 1)
                    pe.matmul(to, w_uh[:], ht_i[:, slot, :], start=True, stop=False, skip_group_check=True)
                    tiles.visit(g, slot % 2, regular, more)

                def body(g, slot, use):
                    if at_least(g, 2):
                        half = slot % 2
                        pe.wait_ge(s_ut, g - 1)
                        if at_least(g, 4):
                            pe.wait_ge(s_fin, g - 3)
                        for j in range(4):
                            ins = pe.matmul(p_out[half][:, j * D:(j + 1) * D], u_t[:, half, j * P:(j + 1) * P],
                                            w_out[:], start=True, stop=True)
                        ins.then_inc(s_o, 1)
                    if below(g, GROUPS):
                        sums(g, slot, use)

                run_steps(pe, GROUPS + 2, 4, GROUPS, 4, body)

            with nc.Block() as block:
                block.sync(sync_2)
                block.gpsimd(gpsimd_2)
                block.vector(vector_2)
                block.scalar(scalar_2)
                block.tensor(tensor_2)


def kernel(**inputs):
    import concourse.bacc as bacc
    from concourse.bass_utils import run_bass_kernel_spmd

    src = np.asarray(inputs["src"]).astype(np.int32)
    dst = np.asarray(inputs["dst"]).astype(np.int32)
    pad = ET * P - E
    both = np.stack([np.pad(a, (0, pad)).reshape(STEPS, 4, P) for a in (src, dst)], 1)
    ends = both.reshape(STEPS, 8, P).transpose(2, 0, 1)
    dst_rows = np.pad(dst, (0, pad), mode="edge").reshape(ET // 2, 2, P)
    dst_cols = np.pad(dst, (0, pad + SPARE * P), constant_values=-1).reshape(ET + SPARE, P).T
    edge_t = np.pad(np.asarray(inputs["edge_attr_32"]), ((0, pad), (0, 0))).T

    def get(name):
        return np.asarray(inputs["L0_gnn_" + name])

    arrays = {
        "x": np.asarray(inputs["x"]), "ends": ends, "dst_rows": dst_rows, "dst_cols": dst_cols, "edge_t": edge_t,
        "wm1": get("Wm1"), "bm1": get("bm1").reshape(D, 1), "wm2": get("Wm2"), "bm2": get("bm2").reshape(D, 1),
        "wu1": get("Wu1"), "bu1": get("bu1").reshape(D, 1), "wu2": get("Wu2"),
        "bu2": np.broadcast_to(get("bu2"), (P, 4, D)).reshape(P, W),
    }
    arrays = {k + "_in": np.ascontiguousarray(v) for k, v in arrays.items()}
    nc = bacc.Bacc("TRN2", target_bir_lowering=False, num_devices=1)
    args = [nc.dram_tensor(k, v.shape, mybir.dt.from_np(v.dtype), kind="ExternalInput").ap() for k, v in arrays.items()]
    out = nc.dram_tensor("out", (N, D), F32, kind="ExternalOutput").ap()
    build(nc, *args, out)
    return run_bass_kernel_spmd(nc, [arrays], core_ids=[0]).results[0]["out"]
```

```python
from contextlib import ExitStack

import numpy as np

import concourse.bass as bass
from concourse import mybir

F32 = mybir.dt.float32
F32R = mybir.dt.float32r
I32 = mybir.dt.int32
ALU = mybir.AluOpType
ACT = mybir.ActivationFunctionType
AX_X = mybir.AxisListType.X

P = 128
N, E, D, DE = 50000, 25000, 128, 32
W = 4 * P
STEPS = -(-E // W)
ET = 4 * STEPS
SPARE = 3
GROUPS = -(-N // W)
LAST = N - W
NEW = (GROUPS - 1) * W
EPS = 1e-5
STAT = 12
TABLE = 18
assert GROUPS == 2 * STEPS and (NEW - LAST) % 4 == 0


def run_steps(eng, total, first, last, unroll, body):
    first, last = -(-first // unroll) * unroll, last // unroll * unroll
    for s in range(first):
        body(s, s % unroll, s // unroll)
    with eng.Fori(first // unroll, last // unroll) as use:
        for slot in range(unroll):
            body(use * unroll + slot, slot, use)
    for s in range(last, total):
        body(s, s % unroll, s // unroll)


def at_least(s, k):
    return not isinstance(s, int) or s >= k


def below(s, k):
    return not isinstance(s, int) or s < k


def build(nc, x, ends, dst_rows, dst_cols, edge_t, wm1, bm1, wm2, bm2, wu1, bu1, wu2, bu2, out):
    with ExitStack() as ctx:
        def sb(name, shape, dt=F32, on=ctx):
            return on.enter_context(nc.sbuf_tensor(name, shape, dt))

        def ps(name, shape, dt=F32):
            return ctx.enter_context(nc.psum_tensor(name, shape, dt))

        def sem(name):
            return ctx.enter_context(nc.semaphore(name))

        ht_d = nc.dram_tensor("ht_scratch", (GROUPS, P, W), F32).ap()
        xh_d = nc.dram_tensor("xh_scratch", (GROUPS, P, W), F32).ap()
        ext_d = nc.dram_tensor("extremes_scratch", (2, ET), F32).ap()
        rng_d = nc.dram_tensor("ranges_scratch", (GROUPS, 2), I32).ap()

        w_src, w_dst, w_msg = sb("w_src", [P, D]), sb("w_dst", [P, D]), sb("w_msg", [P, D])
        w_edge = sb("w_edge", [DE, D])
        w_uh, w_ua, w_out = sb("w_uh", [P, D]), sb("w_ua", [P, D]), sb("w_out", [P, D])
        b_m1, b_m2, b_u1 = sb("b_m1", [P, 1]), sb("b_m2", [P, 1]), sb("b_u1", [P, 1])
        b_out = sb("b_out", [P, W])
        dst_f = sb("dst_f", [P, ET + SPARE])
        node = sb("node", [P, W])
        minus_base = sb("minus_base", [P, GROUPS])
        ranges = sb("ranges", [1, GROUPS * 2], I32)
        msgs = sb("msgs", [P, ET + SPARE, D])
        ht_i, xh_i = sb("ht_i", [P, 4, W]), sb("xh_i", [P, 4, W])
        ht = sb("ht", [P, 2, 4, W])
        xh_o = sb("xh_o", [P, 2, 2, W])
        banks = [ps(f"bank{i}", [P, W]) for i in range(8)]

        s_w = sem("weights_loaded")
        s_idx = sem("indices_loaded")
        s_cst = sem("constants_made")
        s_pre = sem("table_steps")
        s_ext = sem("extremes_moved")
        s_rng = sem("ranges_moved")
        s_xn = [sem(f"nodes_loaded{i}") for i in range(4)]
        s_xg = [sem(f"ends_gathered{i}") for i in range(4)]
        s_cp = sem("ends_copied")
        s_stat = sem("stat")
        s_sd = sem("sd_ready")
        s_zv = sem("z_by_vector")
        s_za = sem("z_by_scalar")
        s_xh = sem("xh_ready")
        s_tr = sem("transposed")
        s_ht = sem("ht_ready")
        s_hus, s_hu = sem("wh_summed"), sem("wh_ready")
        s_m1, s_m2, s_msg = sem("m1_summed"), sem("m2_summed"), sem("msg_summed")
        s_m1t, s_m2t, s_msgs = sem("m1t_ready"), sem("m2t_ready"), sem("msgs_ready")
        s_sto = [sem(f"scratch_stored{i}") for i in range(2)]

        s_ldh = [sem(f"ht_loaded{i}") for i in range(4)]
        s_ldx = [sem(f"xh_loaded{i}") for i in range(4)]
        s_hot, s_hot_x = sem("onehots_ready"), sem("more_onehots_ready")
        s_hi, s_hi_x = sem("high_parts_ready"), sem("more_high_parts_ready")
        s_lo, s_lo_x = sem("low_parts_ready"), sem("more_low_parts_ready")
        s_used = [sem(f"further_tiles_used{i}") for i in range(2)]
        s_agg = sem("u_summed")
        s_sum, s_pre_u = sem("edge_sums_copied"), sem("pre_u_ready")
        s_ut = sem("u_ready")
        s_xb = sem("xh_biased")
        s_sel, s_bias, s_bias_lo = sem("row_sel_steps"), sem("bias_rows_made"), sem("bias_low_made")
        s_o = sem("out_summed")
        s_fin = sem("out_ready")
        s_out = [sem(f"out_stored{i}") for i in range(4)]

        def load_h(sp, g, slot):
            sp.dma_start(ht_i[:, slot, :], ht_d[g]).then_inc(s_ldh[slot], 16)

        def load_xh(sp, g, slot):
            sp.dma_start(xh_i[:, slot, :], xh_d[g]).then_inc(s_ldx[slot], 16)

        with ExitStack() as one:
            ident = sb("ident", [P, P], on=one)
            ends_all = sb("ends_all", [P, STEPS, 8], I32, on=one)
            ends_now = sb("ends_now", [P, 8, 8], I32, on=one)
            dst_i = sb("dst_i", [P, ET + SPARE], I32, on=one)
            minus_i = sb("minus_i", [P, GROUPS], I32, on=one)
            rows_i = sb("rows_i", [ET // 2, 2, P], I32, on=one)
            ext = sb("ext", [ET // 2, 2, 2], on=one)
            base_i = sb("base_i", [GROUPS, 1], I32, on=one)
            first, last = sb("first", [GROUPS, 1], on=one), sb("last", [GROUPS, 1], on=one)
            lo_f, hi_f = sb("lo_f", [GROUPS, 1], on=one), sb("hi_f", [GROUPS, 1], on=one)
            rng_i = sb("rng_i", [GROUPS, 2], I32, on=one)

            xg = sb("xg", [P, 4, 8, D], on=one)
            xn = sb("xn", [P, 4, 8, D], on=one)
            zn = sb("zn", [P, 2, 8, D], on=one)
            edge = sb("edge", [DE, 4, W], on=one)
            bn = sb("bn", [P, 2, 16, 6], on=one)
            pair, diff = sb("pair", [P, 16, 2], on=one), sb("diff", [P, 16], on=one)
            sq, var, sd = (sb(n, [P, 16], on=one) for n in ("sq", "var", "sd"))
            veps, r0, r1, r2 = (sb(n, [P, 16], on=one) for n in ("veps", "r0", "r1", "r2"))
            mean, rstd, shift = (sb(n, [P, 2, 16], on=one) for n in ("mean", "rstd", "shift"))
            m1t, m2t = sb("m1t", [P, W], on=one), sb("m2t", [P, W], on=one)

            spare = zn[:, 0, :, :].rearrange("p t d -> p (t d)")
            ext_all = spare[:, 0:2 * ET].rearrange("p (a k) -> p a k", a=2)
            up_f, down_f = spare[:, 2 * ET:3 * ET], spare[:, 3 * ET:4 * ET]
            spare = zn[:, 1, :, :].rearrange("p t d -> p (t d)")[0:GROUPS]
            reaches, hit = spare[:, 0:ET], spare[:, ET:2 * ET]
            ahead, behind = spare[:, 2 * ET:3 * ET], spare[:, 3 * ET:4 * ET]
            rows_f = xh_o[0:ET // 2, 0, 0, 0:2 * P].rearrange("q (k e) -> q k e", k=2)

            node_i = xh_o[:, 0, 1, :].bitcast(I32)
            up_i, down_i = xh_o[:, 1, 0, 0:ET].bitcast(I32), xh_o[:, 1, 0, ET:2 * ET].bitcast(I32)

            p_tr, (p_m1, p_m2, p_msg, p_hu) = banks[0:4], banks[4:8]

            def sync_1(sp):
                sp.dma_start(ends_all[:], ends).then_inc(s_idx, 16)
                sp.dma_start(rows_i[:], dst_rows).then_inc(s_ext, 16)

                def load_nodes(s, slot):
                    if below(s, STEPS - 1):
                        sp.dma_start(xn[:, slot].rearrange("p (h j) d -> p h (j d)", h=2),
                                     x[bass.ds(s * 2 * W, 2 * W), :].rearrange("(h p j) d -> p h (j d)", h=2, p=P)
                                     ).then_inc(s_xn[slot], 16)
                    else:
                        for h, row in enumerate((s * 2 * W, LAST)):
                            sp.dma_start(xn[:, slot, 4 * h:4 * h + 4],
                                         x[row:row + W, :].rearrange("(p j) d -> p j d", p=P)).then_inc(s_xn[slot], 16)
                    sp.dma_start(edge[:, slot], edge_t[:, bass.ds(s * W, W)]).then_inc(s_xn[slot], 16)

                load_nodes(0, 0)
                sp.dma_start(dst_i[:], dst_cols).then_inc(s_ext, 16)
                sp.dma_start(b_m1[:], bm1).then_inc(s_w, 16)
                sp.dma_start(b_m2[:], bm2).then_inc(s_w, 16)
                sp.dma_start(b_u1[:], bu1).then_inc(s_w, 16)
                sp.wait_ge(s_pre, 3)
                for a in range(2):
                    sp.dma_start(ext_d[a].rearrange("(q k) -> q k", k=2), ext[:, a, :]).then_inc(s_ext, 16)
                load_nodes(1, 1)
                sp.wait_ge(s_ext, 64)
                for a in range(2):
                    sp.dma_start(ext_all[:, a, :], ext_d[a].partition_broadcast(P)).then_inc(s_ext, 16)
                for to, of in ((w_src, wm1[0:D]), (w_dst, wm1[D:2 * D]), (w_edge, wm1[2 * D:2 * D + DE]), (w_msg, wm2),
                               (w_ua, wu1[D:2 * D])):
                    sp.dma_start(to[:], of).then_inc(s_w, 16)
                load_nodes(2, 2)
                load_nodes(3, 3)
                for to, of in ((w_uh, wu1[0:D]), (w_out, wu2), (b_out, bu2)):
                    sp.dma_start(to[:], of).then_inc(s_w, 16)
                sp.wait_ge(s_pre, TABLE)
                sp.dma_start(rng_d, rng_i[:]).then_inc(s_rng, 16)
                sp.wait_ge(s_rng, 16)
                sp.dma_start(ranges[:], rng_d.rearrange("(o g) c -> o (g c)", o=1)).then_inc(s_rng, 16)

                def body(s, slot, use):
                    if not below(s, STEPS - 1) and below(s, STEPS + 1):
                        for g in range(2 * (s - STEPS + 1), 2 * (s - STEPS + 2)):
                            load_h(sp, g, g)
                            load_xh(sp, g, g)
                    if below(s, STEPS - 1) and at_least(s, 3):
                        sp.wait_ge(s_xh, 2 * (s - 2))
                        sp.wait_ge(s_m1, s - 2)
                        load_nodes(s + 1, (slot + 1) % 4)
                    if at_least(s, 3):
                        to, half = bass.ds(2 * (s - 3), 2), (slot + 1) % 2
                        sp.wait_ge(s_ht, 4 * (s - 2))
                        sp.wait_ge(s_hu, s - 2)
                        sp.dma_start(ht_d[to].rearrange("g p f -> p g f"), ht[:, half, 2:4]).then_inc(s_sto[half], 16)
                        sp.wait_ge(s_xh, 2 * (s - 2))
                        sp.dma_start(xh_d[to].rearrange("g p f -> p g f"), xh_o[:, half]).then_inc(s_sto[half], 16)

                run_steps(sp, STEPS + 3, 4, STEPS - 2, 4, body)
                sp.wait_ge(s_rng, 32)

            def gpsimd_1(pool):
                pool.iota(base_i[:], [[0, 1]], base=0, channel_multiplier=W).then_inc(s_cst, 1)
                pool.iota(up_i, [[1, ET]], base=1, channel_multiplier=0).then_inc(s_cst, 1)
                pool.iota(down_i, [[-1, ET]], base=ET, channel_multiplier=0).then_inc(s_cst, 1)
                pool.iota(node_i, [[1, 4], [4, P]], base=0, channel_multiplier=0).then_inc(s_cst, 1)
                pool.iota(minus_i[:], [[-W, GROUPS]], base=0, channel_multiplier=0).then_inc(s_cst, 1)
                pool.memset(ident[:], 0.0).then_inc(s_cst, 1)
                pool.memset(msgs[:, ET:, :], 0.0).then_inc(s_cst, 1)
                pool.wait_ge(s_idx, 16)
                pool.tensor_copy(ends_now[:, 0:4], ends_all[:, 0:4, :]).then_inc(s_cp, 1)
                pool.wait_ge(s_cp, 1)

                def body(s, slot8, use8):
                    slot = slot8 % 4
                    if slot % 2 == 1 and at_least(s, 3):
                        pool.wait_ge(s_tr, 4 * (s - 2) - 2)
                        pool.wait_ge(s_cp, 4 * use8 + (slot8 + 1) // 2)
                        if at_least(s, 5):
                            pool.wait_ge(s_xg[slot - 1], 128 * (2 * use8 + slot8 // 4))
                            pool.wait_ge(s_xg[slot], 128 * (2 * use8 + slot8 // 4))
                    if slot % 2 == 1 and below(s, STEPS - 3):
                        n = 2 if below(s, STEPS - 4) else 1
                        to = (slot8 + 3) % 8
                        pool.tensor_copy(ends_now[:, to:to + n], ends_all[:, bass.ds(s + 3, n), :]).then_inc(s_cp, 1)
                    for t in range(8):
                        pool.indirect_dma_start(
                            xg[:, slot, t, :], None, x,
                            bass.IndirectOffsetOnAxis(ap=ends_now[:, slot8, t:t + 1], axis=0)).then_inc(s_xg[slot], 16)
                    if not at_least(s, 1):
                        pool.wait_ge(s_cst, 6)
                        pool.affine_select(out=ident[:], in_=ident[:], compare_op=ALU.not_equal, fill=1.0, base=0,
                                           pattern=[[-1, P]], channel_multiplier=1).then_inc(s_cst, 1)

                run_steps(pool, STEPS, 8, STEPS - 4, 8, body)

            def start_table(dve, did):
                dve.wait_ge(s_ext, 32)
                did(dve.tensor_copy(rows_f, rows_i[:]))
                did(dve.tensor_reduce(ext[:, 0, :], rows_f, AX_X, ALU.min), False)
                did(dve.tensor_reduce(ext[:, 1, :], rows_f, AX_X, ALU.max), False)
                did(dve.tensor_copy(dst_f[:], dst_i[:]), False)
                dve.wait_ge(s_cst, 5)
                did(dve.tensor_copy(node[:], node_i), False)
                did(dve.tensor_copy(minus_base[:], minus_i[:]), False)
                did(dve.tensor_copy(up_f, up_i), False)
                did(dve.tensor_copy(down_f, down_i))
                did(dve.memset(minus_base[:, GROUPS - 1:GROUPS], -float(LAST)), False)
                did(dve.tensor_scalar(first[:], base_i[:], float(LAST), None, ALU.min), False)
                did(dve.tensor_scalar(last[:], base_i[:], float(LAST), float(W - 1), ALU.min, ALU.add))

            def finish_table(dve, did):
                dve.wait_ge(s_ext, 96)
                did(dve.tensor_scalar(reaches, ext_all[0:GROUPS, 1, :], first[:], None, ALU.is_ge))
                did(dve.scalar_tensor_tensor(out=hit, in0=ext_all[0:GROUPS, 0, :], scalar=last[:],
                                             in1=reaches, op0=ALU.is_le, op1=ALU.mult))
                dve.tensor_tensor(ahead, hit, up_f[0:GROUPS], ALU.mult)
                did(dve.tensor_tensor(behind, hit, down_f[0:GROUPS], ALU.mult))
                dve.tensor_reduce(hi_f[:], ahead, AX_X, ALU.max)
                did(dve.tensor_reduce(lo_f[:], behind, AX_X, ALU.max))
                did(dve.tensor_scalar(r0[0:GROUPS, 0:1], lo_f[:], 2.0, None, ALU.max))
                dve.tensor_scalar(rng_i[:, 0:1], r0[0:GROUPS, 0:1], -1.0, float(ET), ALU.mult, ALU.add)
                did(dve.tensor_scalar(r1[0:GROUPS, 0:1], r0[0:GROUPS, 0:1], -1.0, float(ET + 2), ALU.mult, ALU.add))
                did(dve.tensor_tensor(rng_i[:, 1:2], r1[0:GROUPS, 0:1], hi_f[:], ALU.max))

            VECTOR_TILES = 9
            assert 8 < VECTOR_TILES < 12

            def vector_1(dve):
                steps = [0]

                def did(ins, wait=True):
                    steps[0] += 1
                    ins.then_inc(s_pre, 1)
                    if wait:
                        dve.wait_ge(s_pre, steps[0])

                start_table(dve, did)

                def stat_of_nodes(s, slot, t):
                    dve.bn_stats(bn[:, slot % 2, 8 + t, :], xn[:, slot, t, :])

                def stat_of_ends(s, slot, use):
                    dve.wait_ge(s_xg[slot], 128 * use + 128)
                    for t in range(8):
                        ins = dve.bn_stats(bn[:, slot % 2, t, :], xg[:, slot, t, :])
                    ins.then_inc(s_stat, 1)

                def statistics(s, slot, between):
                    half = slot % 2
                    if at_least(s, 2):
                        dve.wait_ge(s_za, 2 * (s - 1))
                        dve.wait_ge(s_zv, 3 * (s - 1))
                    dve.wait_ge(s_stat, STAT * s + 1)
                    dve.tensor_tensor(pair[:], bn[:, half, :, 1:3], bn[:, half, :, 4:6], ALU.add).then_inc(s_stat, 1)
                    dve.tensor_tensor(diff[:], bn[:, half, :, 1], bn[:, half, :, 4], ALU.subtract).then_inc(s_stat, 1)
                    between(0)
                    dve.wait_ge(s_stat, STAT * s + 3)
                    dve.scalar_tensor_tensor(out=sq[:], in0=diff[:], scalar=0.25, in1=diff[:], op0=ALU.mult,
                                             op1=ALU.mult).then_inc(s_stat, 1)
                    dve.tensor_scalar(mean[:, half], pair[:, :, 0], 0.5, None, ALU.mult).then_inc(s_stat, 1)
                    between(1)
                    dve.wait_ge(s_stat, STAT * s + 5)
                    dve.scalar_tensor_tensor(out=var[:], in0=pair[:, :, 1], scalar=1.0 / D, in1=sq[:], op0=ALU.mult,
                                             op1=ALU.add).then_inc(s_stat, 1)
                    between(2)
                    dve.wait_ge(s_stat, STAT * s + 6)
                    dve.tensor_scalar(veps[:], var[:], EPS, None, ALU.add).then_inc(s_stat, 1)
                    for i in range(3, 6):
                        between(i)
                    dve.wait_ge(s_sd, s + 1)
                    dve.reciprocal(r0[:], sd[:]).then_inc(s_stat, 1)
                    between(6)
                    dve.wait_ge(s_stat, STAT * s + 8)
                    dve.scalar_tensor_tensor(out=r1[:], in0=r0[:], scalar=-0.5, in1=r0[:], op0=ALU.mult,
                                             op1=ALU.mult).then_inc(s_stat, 1)
                    between(7)
                    dve.wait_ge(s_stat, STAT * s + 9)
                    dve.tensor_tensor(r2[:], r1[:], veps[:], ALU.mult).then_inc(s_stat, 1)
                    between(8)
                    dve.wait_ge(s_stat, STAT * s + 10)
                    dve.scalar_tensor_tensor(out=rstd[:, half], in0=r2[:], scalar=1.5, in1=r0[:], op0=ALU.add,
                                             op1=ALU.mult).then_inc(s_stat, 1)
                    between(9)
                    dve.wait_ge(s_stat, STAT * s + 11)
                    dve.scalar_tensor_tensor(out=shift[:, half], in0=mean[:, half], scalar=-1.0, in1=rstd[:, half], op0=ALU.mult,
                                             op1=ALU.mult).then_inc(s_stat, 1)

                def x_plus_h(s, slot, h):
                    half = slot % 2
                    dve.scalar_tensor_tensor(
                        out=xh_o[:, half, h, :].rearrange("p (j d) -> p j d", j=4), in0=zn[:, half, 4 * h:4 * h + 4, :],
                        scalar=0.0, in1=xn[:, slot, 4 * h:4 * h + 4, :], op0=ALU.max, op1=ALU.add).then_inc(s_xh, 1)

                def normalise(s, slot):
                    if at_least(s, 2):
                        dve.wait_ge(s_tr, 4 * (s - 1))
                        dve.wait_ge(s_xh, 2 * (s - 1))
                    for t in range(VECTOR_TILES):
                        if t < 8:
                            of = to = xg[:, slot, t, :]
                        else:
                            of, to = xn[:, slot, t - 8, :], zn[:, slot % 2, t - 8, :]
                        ins = dve.tensor_scalar(to, of, mean[:, slot % 2, t:t + 1], rstd[:, slot % 2, t:t + 1],
                                                ALU.subtract, ALU.mult)
                        if t in (3, 7, VECTOR_TILES - 1):
                            ins.then_inc(s_zv, 1)

                def body(s, slot, use):
                    prev, prev2 = (slot - 1) % 4, (slot - 2) % 4
                    if below(s, STEPS):
                        dve.wait_ge(s_xn[slot], 32 * use + 32 + (0 if below(s, STEPS - 1) else 16))
                    def between(i):
                        if i < 8 and below(s, STEPS):
                            stat_of_nodes(s, slot, i)
                        if i == 8 and at_least(s, 2):
                            dve.wait_ge(s_za, 2 * (s - 1))
                            dve.wait_ge(s_zv, 3 * (s - 1))
                            if at_least(s, 4):
                                dve.wait_ge(s_sto[slot % 2], 64 * use + (32 if slot >= 2 else 0) - 32)
                        if i >= 8 and at_least(s, 2):
                            x_plus_h(s - 2, prev2, i - 8)

                    if at_least(s, 1) and below(s, STEPS + 1):
                        statistics(s - 1, prev, between)
                        normalise(s - 1, prev)
                    else:
                        for i in range(10):
                            between(i)
                    if not at_least(s, 1):
                        finish_table(dve, did)
                        assert steps[0] == TABLE
                    if below(s, STEPS):
                        stat_of_ends(s, slot, use)

                run_steps(dve, STEPS + 2, 4, STEPS - 1, 4, body)

            def scalar_1(act):
                act.wait_ge(s_w, 16 * 11)

                def body(s, slot, use):
                    has_norm = at_least(s, 1) and below(s, STEPS + 1)
                    has_msg = at_least(s, 2)
                    prev = (slot - 1) % 4

                    def normalise(tiles):
                        for t in tiles:
                            ins = act.activation(zn[:, prev % 2, t - 8, :], xn[:, prev, t - 8, :], ACT.Identity,
                                                 bias=shift[:, prev % 2, t:t + 1], scale=rstd[:, prev % 2, t:t + 1])
                        ins.then_inc(s_za, 1)

                    def relu(qs):
                        for q in qs:
                            act.wait_ge(s_tr, 4 * (s - 1) + q + 1)
                            act.activation(ht[:, prev % 2, q, :], p_tr[q][:], ACT.Relu).then_inc(s_ht, 1)

                    def w_h(s, half):
                        act.wait_ge(s_hus, s + 1)
                        act.activation(ht[:, half, 2, :], p_hu[:], ACT.Copy).then_inc(s_hu, 1)

                    if has_norm:
                        act.wait_ge(s_stat, STAT * (s - 1) + 7)
                        act.activation(sd[:], veps[:], ACT.Sqrt).then_inc(s_sd, 1)
                    if at_least(s, 3):
                        w_h(s - 3, (slot - 3) % 2)
                    if has_msg:
                        act.wait_ge(s_m1, s - 1)
                        act.activation(m1t[:], p_m1[:], ACT.Relu, bias=b_m1[:]).then_inc(s_m1t, 1)
                        if not below(s, STEPS + 1):
                            w_h(s - 2, slot % 2)
                    if has_norm:
                        act.wait_ge(s_stat, STAT * (s - 1) + 12)
                        normalise(range(VECTOR_TILES, 12))
                    if has_msg:
                        act.wait_ge(s_m2, s - 1)
                        act.activation(m2t[:], p_m2[:], ACT.Relu, bias=b_m2[:]).then_inc(s_m2t, 1)
                    if has_norm:
                        normalise(range(12, 16))
                    if has_norm:
                        relu(range(2))
                    if has_msg:
                        act.wait_ge(s_msg, s - 1)
                        act.activation(msgs[:, bass.ds(4 * (s - 2), 4), :], p_msg[:].rearrange("p (j d) -> p j d", j=4),
                                       ACT.Copy).then_inc(s_msgs, 1)
                    if has_norm:
                        if at_least(s, 3):
                            act.wait_ge(s_sto[prev % 2], 64 * use + (-32, 0, 0, 32)[slot])
                        relu(range(2, 4))

                run_steps(act, STEPS + 2, 4, STEPS - 1, 4, body)

            def tensor_1(pe):
                pe.wait_ge(s_w, 16 * 11)
                pe.wait_ge(s_cst, 8)

                def transposes(s, slot, qs):
                    for q in qs:
                        pe.wait_ge(s_zv, 3 * s + min(q, 2) + 1)
                        if q >= 2:
                            pe.wait_ge(s_za, 2 * s + q - 1)
                        if at_least(s, 1):
                            pe.wait_ge(s_ht, 4 * (s - 1) + q + 1)
                        for j in range(4):
                            of = xg[:, slot, 4 * q + j, :] if q < 2 else zn[:, slot % 2, 4 * (q - 2) + j, :]
                            ins = pe.transpose(p_tr[q][:, j * P:(j + 1) * P], of, ident[:])
                        ins.then_inc(s_tr, 1)

                def messages(s, slot, use, part):
                    if part == 0:
                        pe.wait_ge(s_ht, 4 * s + 2)
                        pe.wait_ge(s_xn[slot], 32 * use + 32 + (0 if below(s, STEPS - 1) else 16))
                        if at_least(s, 1):
                            pe.wait_ge(s_m1t, s)
                        pe.matmul(p_m1[:], w_src[:], ht[:, slot % 2, 0, :], start=True, stop=False)
                        pe.matmul(p_m1[:], w_dst[:], ht[:, slot % 2, 1, :], start=False, stop=False)
                        pe.matmul(p_m1[:], w_edge[:], edge[:, slot, :], start=False, stop=True).then_inc(s_m1, 1)
                        pe.wait_ge(s_ht, 4 * s + 3)
                        if at_least(s, 1):
                            pe.wait_ge(s_hu, s)
                        pe.matmul(p_hu[:], w_uh[:], ht[:, slot % 2, 2, :], start=True, stop=True).then_inc(s_hus, 1)
                    if part == 1:
                        pe.wait_ge(s_m1t, s + 1)
                        pe.matmul(p_m2[:], w_msg[:], m1t[:], start=True, stop=True).then_inc(s_m2, 1)
                    if part == 2:
                        pe.wait_ge(s_m2t, s + 1)
                        if at_least(s, 1):
                            pe.wait_ge(s_msgs, s)
                        for j in range(4):
                            ins = pe.matmul(p_msg[:, j * D:(j + 1) * D], m2t[:, j * P:(j + 1) * P], w_ua[:],
                                            start=True, stop=True)
                        ins.then_inc(s_msg, 1)

                def body(s, slot, use):
                    prev, prev2 = (slot - 1) % 4, (slot - 2) % 4
                    for part, qs in enumerate(((), (0, 1), (2, 3))):
                        if at_least(s, 2):
                            messages(s - 2, prev2, use - (slot < 2), part)
                        if at_least(s, 1) and below(s, STEPS + 1):
                            transposes(s - 1, prev, qs)

                run_steps(pe, STEPS + 2, 4, STEPS - 1, 4, body)

            with nc.Block() as block:
                block.sync(sync_1)
                block.gpsimd(gpsimd_1)
                block.vector(vector_1)
                block.scalar(scalar_1)
                block.tensor(tensor_1)

        with ExitStack() as two:
            hot = sb("hot", [P, 10, W], F32R, on=two)
            high, low = sb("high", [P, 10, D], F32R, on=two), sb("low", [P, 10, D], F32R, on=two)
            pre_u = sb("pre_u", [P, W], on=two)
            u_t = sb("u_t", [P, 2, W], on=two)
            bias_rows, row_sel = sb("bias_rows", [P, W], F32R, on=two), sb("row_sel", [P, P], F32R, on=two)
            row_sel_f = sb("row_sel_f", [P, P], on=two)
            out_o = sb("out_o", [P, 4, W], on=two)
            p_agg, p_out = banks[0:2], banks[2:4]

            def sync_2(sp):
                for half in range(2):
                    sp.wait_ge(s_sto[half], 32 * ((STEPS + 1 - half) // 2))

                def store(g, slot):
                    sp.wait_ge(s_fin, g + 1)
                    if below(g, GROUPS - 1):
                        rows, of = out[bass.ds(g * W, W), :], out_o[:, slot, :]
                    else:
                        rows, of = out[NEW:N, :], out_o[(NEW - LAST) // 4:P, slot, :]
                    sp.dma_start(rows.rearrange("(p j) d -> p (j d)", j=4), of).then_inc(s_out[slot], 16)

                def body(g, slot, use):
                    if at_least(g, 3) and below(g, GROUPS - 1):
                        if slot % 2 == 1:
                            sp.wait_ge(s_pre_u, 2 * use + slot // 2)
                        else:
                            sp.wait_ge(s_agg, g - 2)
                        load_h(sp, g + 1, (slot + 1) % 4)
                    if below(g, GROUPS) and at_least(g, 4):
                        sp.wait_ge(s_fin, g - 3)
                        load_xh(sp, g, slot)
                    if at_least(g, 4):
                        store(g - 4, slot)

                run_steps(sp, GROUPS + 4, 4, GROUPS, 4, body)
                for slot in range(4):
                    sp.wait_ge(s_out[slot], 16 * len(range(slot, GROUPS, 4)))

            class EdgeTiles:

                def __init__(self, eng, name):
                    self.eng = eng
                    self.regs = [eng.alloc_register(f"{name}_range{i}") for i in range(2)]
                    self.count = eng.alloc_register(f"{name}_count")
                    eng.reg_mov(self.count, 0)
                    self.in_pair = [eng.alloc_register(f"{name}_in_pair{i}") for i in range(2)]
                    for count in self.in_pair:
                        eng.reg_mov(count, 1)

                def up_to(self):
                    self.eng.reg_add(self.count, self.count, 1)
                    return self.eng.snap(self.count, min_val=1, max_val=GROUPS * ET)

                def wait_for_slot(self, pair):
                    count = self.in_pair[pair]
                    self.eng.wait_ge(s_used[pair], self.eng.snap(count, min_val=1, max_val=GROUPS * ET))
                    self.eng.reg_add(count, count, 1)

                def visit(self, g, par, regular, more):
                    eng = self.eng
                    eng.load(self.regs, ranges[0:1, bass.ds(g * 2, 2)])
                    lo = eng.snap(self.regs[0], min_val=0, max_val=ET - 2)
                    hi = eng.snap(self.regs[1], min_val=2, max_val=ET)
                    regular(lo, 2 * par, 0)
                    with eng.If(hi > lo + 2):
                        more(lo + 2, 4 + par, None)
                        with eng.If(hi > lo + 3):
                            with eng.Fori(lo + 3, hi, 4) as k:
                                more(k, 6, 0)
                                more(k + 1, 7, 0)
                                with eng.If(hi > k + 2):
                                    more(k + 2, 8, 1)
                                    more(k + 3, 9, 1)
                    regular(lo + 1, 2 * par + 1, 1)

            def gpsimd_2(pool):
                tiles = EdgeTiles(pool, "pool")

                def bias_low():
                    pool.memset(row_sel_f[:], 0.0).then_inc(s_sel, 1)
                    pool.wait_ge(s_sel, 1)
                    pool.memset(row_sel_f[0:1], 1.0).then_inc(s_sel, 1)
                    pool.wait_ge(s_sel, 2)
                    pool.memset(row_sel_f[P // 2:P // 2 + 1], 1.0).then_inc(s_sel, 1)
                    pool.wait_ge(s_sel, 3)
                    pool.wait_ge(s_bias, 1)
                    pool.tensor_tensor(bias_rows[P // 2:P], b_out[P // 2:P], bias_rows[P // 2:P].bitcast(F32), ALU.subtract
                                       ).then_inc(s_bias_lo, 1)
                    pool.wait_ge(s_bias_lo, 1)

                def low_parts(g, slot):
                    def part(k, at):
                        return pool.tensor_tensor(low[:, at, :], msgs[:, k, :], high[:, at, :].bitcast(F32), ALU.subtract)

                    def regular(k, at, n):
                        pool.wait_ge(s_hi, 2 * g + n + 1)
                        part(k, at).then_inc(s_lo, 1)

                    def more(k, at, pair):
                        pool.wait_ge(s_hi_x, tiles.up_to())
                        part(k, at).then_inc(s_lo_x, 1)

                    tiles.visit(g, slot % 2, regular, more)

                def body(g, slot, use):
                    if below(g, GROUPS):
                        low_parts(g, slot)
                    if not at_least(g, 1):
                        bias_low()
                    prev = (slot - 1) % 4
                    if slot % 2 == 1:
                        pool.wait_ge(s_sum, 2 * use + slot // 2 + 1)
                        pool.wait_ge(s_ldh[prev], 16 * use + 16)
                        pool.tensor_tensor(pre_u[:], pre_u[:], ht_i[:, prev, :], ALU.add).then_inc(s_pre_u, 1)
                    elif at_least(g, 2):
                        pool.wait_ge(s_ldx[prev], 16 * (use - (slot < 1)) + 16)
                        pool.tensor_tensor(xh_i[:, prev, :], xh_i[:, prev, :], b_out[:], ALU.add).then_inc(s_xb, 1)

                run_steps(pool, GROUPS + 1, 4, GROUPS, 4, body)

            def vector_2(dve):
                tiles = EdgeTiles(dve, "dve")

                def onehots(g, slot):
                    def onehot(k, at):
                        return dve.tensor_scalar(hot[:, at, :], node[:], dst_f[:, bass.ds(k, 1)],
                                                 minus_base[:, bass.ds(g, 1)], ALU.subtract, ALU.is_equal)

                    def regular(k, at, n):
                        onehot(k, at).then_inc(s_hot, 1)

                    def more(k, at, pair):
                        if pair is not None:
                            tiles.wait_for_slot(pair)
                        tiles.up_to()
                        onehot(k, at).then_inc(s_hot_x, 1)

                    if at_least(g, 2):
                        dve.wait_ge(s_agg, g - 1)
                    tiles.visit(g, slot % 2, regular, more)

                def finish(g, slot, use, odd_before):
                    dve.wait_ge(s_o, g + 1)
                    if slot % 2 == 1:
                        dve.wait_ge(s_xb, odd_before + 1)
                    else:
                        dve.wait_ge(s_ldx[slot], 16 * use + 16)
                    if at_least(g, 4):
                        dve.wait_ge(s_out[slot], 16 * use)
                    dve.tensor_tensor(out_o[:, slot, :], p_out[slot % 2][:], xh_i[:, slot, :], ALU.add
                                      ).then_inc(s_fin, 1)

                def body(g, slot, use):
                    if below(g, GROUPS):
                        onehots(g, slot)
                    if at_least(g, 3):
                        finish(g - 3, (slot - 3) % 4, use - (slot < 3), 2 * use + slot // 2 - 2)

                run_steps(dve, GROUPS + 3, 8, GROUPS, 4, body)

            def scalar_2(act):
                tiles = EdgeTiles(act, "act")

                def high_parts(g, slot):
                    def part(k, at):
                        return act.activation(high[:, at, :], msgs[:, k, :], ACT.Copy)

                    def regular(k, at, n):
                        part(k, at).then_inc(s_hi, 1)

                    def more(k, at, pair):
                        if pair is not None:
                            tiles.wait_for_slot(pair)
                        tiles.up_to()
                        part(k, at).then_inc(s_hi_x, 1)

                    if at_least(g, 2):
                        act.wait_ge(s_agg, g - 1)
                    tiles.visit(g, slot % 2, regular, more)

                def u_of(g, half, of):
                    if at_least(g, 2):
                        act.wait_ge(s_o, g - 1)
                    act.activation(u_t[:, half, :], of, ACT.Relu, bias=b_u1[:]).then_inc(s_ut, 1)

                def body(g, slot, use):
                    if below(g, GROUPS):
                        high_parts(g, slot)
                    if not at_least(g, 1):
                        act.activation(bias_rows[:], b_out[:], ACT.Copy).then_inc(s_bias, 1)
                        act.wait_ge(s_sel, 3)
                        act.activation(row_sel[:], row_sel_f[:], ACT.Copy).then_inc(s_bias, 1)
                    if slot == 1:
                        act.wait_ge(s_agg, g)
                        if at_least(g, 3):
                            act.wait_ge(s_ut, g - 2)
                        act.activation(pre_u[:], p_agg[0][:], ACT.Copy).then_inc(s_sum, 1)
                    elif at_least(g, 2):
                        act.wait_ge(s_pre_u, use)
                        u_of(g - 2, 0, pre_u[:])
                        act.wait_ge(s_agg, g)
                        u_of(g - 1, 1, p_agg[1][:])

                run_steps(act, GROUPS + 1, 4, GROUPS, 2, body)

            def tensor_2(pe):
                tiles = EdgeTiles(pe, "pe")
                for pair in range(2):
                    pe.matmul(p_out[0][:, 0:D], w_out[:], w_out[:], start=True, stop=True).then_inc(s_used[pair], 2)

                def sums(g, slot, use):
                    to = p_agg[slot % 2][:]
                    even = slot % 2 == 0

                    def add(at, stop, start=False):
                        pe.matmul(to, low[:, at, :], hot[:, at, :], start=start, stop=False, skip_group_check=True)
                        return pe.matmul(to, high[:, at, :], hot[:, at, :], start=False, stop=stop,
                                         skip_group_check=True)

                    def regular(k, at, n):
                        pe.wait_ge(s_hot, 2 * g + n + 1)
                        pe.wait_ge(s_lo, 2 * g + n + 1)
                        ins = add(at, n == 1, n == 0 and even)
                        if n == 1:
                            ins.then_inc(s_agg, 1)

                    def more(k, at, pair):
                        count = tiles.up_to()
                        pe.wait_ge(s_hot_x, count)
                        pe.wait_ge(s_lo_x, count)
                        ins = add(at, False)
                        if pair is not None:
                            ins.then_inc(s_used[pair], 1)

                    if even:
                        if at_least(g, 2):
                            pe.wait_ge(s_sum, 2 * use + slot // 2)
                    else:
                        pe.wait_ge(s_ldh[slot], 16 * use + 16)
                        if at_least(g, 2):
                            pe.wait_ge(s_ut, g - 1)
                        pe.matmul(to, w_uh[:], ht_i[:, slot, :], start=True, stop=False, skip_group_check=True)
                    tiles.visit(g, slot % 2, regular, more)

                def outs(g, half):
                    pe.wait_ge(s_ut, g + 1)
                    if at_least(g, 2):
                        pe.wait_ge(s_fin, g - 1)
                    even = half == 0
                    if even:
                        if not at_least(g, 1):
                            pe.wait_ge(s_bias, 2)
                            pe.wait_ge(s_bias_lo, 1)
                        pe.matmul(p_out[half][:], row_sel[:], bias_rows[:], start=True, stop=False,
                                  skip_group_check=True)
                    for j in range(4):
                        ins = pe.matmul(p_out[half][:, j * D:(j + 1) * D], u_t[:, half, j * P:(j + 1) * P],
                                        w_out[:], start=not even, stop=True, skip_group_check=True)
                    ins.then_inc(s_o, 1)

                def body(g, slot, use):
                    if at_least(g, 3):
                        outs(g - 3, (slot - 3) % 2)
                    if below(g, GROUPS):
                        sums(g, slot, use)

                run_steps(pe, GROUPS + 3, 4, GROUPS, 4, body)

            with nc.Block() as block:
                block.sync(sync_2)
                block.gpsimd(gpsimd_2)
                block.vector(vector_2)
                block.scalar(scalar_2)
                block.tensor(tensor_2)


def kernel(**inputs):
    import concourse.bacc as bacc
    from concourse.bass_utils import run_bass_kernel_spmd

    src, dst = np.asarray(inputs["src"]), np.asarray(inputs["dst"])
    pad = ET * P - E
    both = np.stack([np.pad(a, (0, pad)).reshape(STEPS, 4, P) for a in (src, dst)], 1)
    ends = both.reshape(STEPS, 8, P).transpose(2, 0, 1)
    dst_rows = np.pad(dst, (0, pad), mode="edge").reshape(ET // 2, 2, P)
    dst_cols = np.pad(dst, (0, pad + SPARE * P), constant_values=-1).reshape(ET + SPARE, P).T
    edge_t = np.pad(np.asarray(inputs["edge_attr_32"]), ((0, pad), (0, 0))).T

    def get(name):
        return np.asarray(inputs["L0_gnn_" + name])

    arrays = {
        "x": np.asarray(inputs["x"]), "ends": ends, "dst_rows": dst_rows, "dst_cols": dst_cols, "edge_t": edge_t,
        "wm1": get("Wm1"), "bm1": get("bm1").reshape(D, 1), "wm2": get("Wm2"), "bm2": get("bm2").reshape(D, 1),
        "wu1": get("Wu1"), "bu1": get("bu1").reshape(D, 1), "wu2": get("Wu2"),
        "bu2": np.broadcast_to(get("bu2"), (P, 4, D)).reshape(P, W),
    }
    arrays = {k + "_in": np.ascontiguousarray(v) for k, v in arrays.items()}
    nc = bacc.Bacc("TRN2", target_bir_lowering=False, num_devices=1)
    args = [nc.dram_tensor(k, v.shape, mybir.dt.from_np(v.dtype), kind="ExternalInput").ap() for k, v in arrays.items()]
    out = nc.dram_tensor("out", (N, D), F32, kind="ExternalOutput").ap()
    build(nc, *args, out)
    return run_bass_kernel_spmd(nc, [arrays], core_ids=[0]).results[0]["out"]
```
